# Optimizing a Trainium2 kernel written in Bass

```python
import numpy as np
import jax
import jax.numpy as jnp

def _softmax(x, axis=-1):
    return jax.nn.softmax(x, axis=axis)

def _gelu(x):
    return jax.nn.gelu(x, approximate=True)

def _silu(x):
    return jax.nn.silu(x)

def _sigmoid(x):
    return jax.nn.sigmoid(x)

def _layernorm(x, axis=-1, eps=1e-05):
    m = jnp.mean(x, axis=axis, keepdims=True)
    v = jnp.var(x, axis=axis, keepdims=True)
    return (x - m) / jnp.sqrt(v + eps)

def _scatter_add(tgt, idx, src, axis=0):
    return tgt.at[idx].add(src)

def _segment_sum(src, seg, n):
    return jax.ops.segment_sum(src, seg, n)
kernel_name = 'mk_conv_seq_d2_conv_nhwc384_r4_5e7eb7'

def setup_inputs(seed: int=0):
    np.random.seed(seed)
    _w = jnp.asarray

    def _rec_inputs():
        import jax
        import jax.numpy as jnp
        _gk = jax.random.key(seed)
        x = -0.0001476 + 0.9999 * jax.random.normal(jax.random.fold_in(_gk, 1), (32, 56, 56, 96), jnp.float32)
        return x
    x = _rec_inputs()

    def _L0_conv_setup():
        import jax, jax.numpy as jnp
        import numpy as np
        WS = 7
        SS = 3
        NH = 4
        EPS = 1e-05

        def _rel_pos_index(ws):
            coords = np.stack(np.meshgrid(np.arange(ws), np.arange(ws), indexing='ij')).reshape(2, -1)
            rel = coords[:, :, None] - coords[:, None, :]
            rel = rel.transpose(1, 2, 0).astype(np.int64)
            rel[..., 0] += ws - 1
            rel[..., 1] += ws - 1
            rel[..., 0] *= 2 * ws - 1
            return rel.sum(-1)

        def _shift_mask(H, W, ws, ss):
            img = np.zeros((H, W), dtype=np.float32)
            cnt = 0
            for h in (slice(0, -ws), slice(-ws, -ss), slice(-ss, None)):
                for w in (slice(0, -ws), slice(-ws, -ss), slice(-ss, None)):
                    img[h, w] = cnt
                    cnt += 1
            mw = img.reshape(H // ws, ws, W // ws, ws).transpose(0, 2, 1, 3).reshape(-1, ws * ws)
            diff = mw[:, None, :] - mw[:, :, None]
            return np.where(diff != 0, -100.0, 0.0).astype(np.float32)

        def _ln(x, g, b):
            m = jnp.mean(x, axis=-1, keepdims=True)
            v = jnp.mean(jnp.square(x - m), axis=-1, keepdims=True)
            return (x - m) * jax.lax.rsqrt(v + EPS) * g + b
        key = jax.random.key(seed)
        ks = jax.random.split(key, 8)
        B, H, W, C = (32, 56, 56, 96)
        D = 4 * C
        s = lambda n: 0.02
        return {'x': jax.random.normal(ks[0], (B, H, W, C), jnp.float32), 'ln1_g': jnp.ones((C,), jnp.float32), 'ln1_b': jnp.zeros((C,), jnp.float32), 'qkv_w': jax.random.normal(ks[1], (C, 3 * C), jnp.float32) * s(C), 'qkv_b': jnp.zeros((3 * C,), jnp.float32), 'proj_w': jax.random.normal(ks[2], (C, C), jnp.float32) * s(C), 'proj_b': jnp.zeros((C,), jnp.float32), 'rpb_table': jax.random.normal(ks[3], ((2 * WS - 1) ** 2, NH), jnp.float32) * 0.02, 'ln2_g': jnp.ones((C,), jnp.float32), 'ln2_b': jnp.zeros((C,), jnp.float32), 'fc1_w': jax.random.normal(ks[4], (C, D), jnp.float32) * s(C), 'fc1_b': jnp.zeros((D,), jnp.float32), 'ln3_g': jnp.ones((D,), jnp.float32), 'ln3_b': jnp.zeros((D,), jnp.float32), 'fc2_w': jax.random.normal(ks[5], (D, C), jnp.float32) * s(D), 'fc2_b': jnp.zeros((C,), jnp.float32)}
    _L0_conv_all = _L0_conv_setup()
    _L0_conv_in = {k: v for k, v in _L0_conv_all.items() if k in ('ln1_g', 'ln1_b', 'qkv_w', 'qkv_b', 'proj_w', 'proj_b', 'rpb_table', 'ln2_g', 'ln2_b', 'fc1_w', 'fc1_b', 'ln3_g', 'ln3_b', 'fc2_w', 'fc2_b')}
    del _L0_conv_all

    def _L1_conv_setup():
        import jax, jax.numpy as jnp
        import numpy as np
        DIM = 96
        NH = 12
        WS = (7, 7)
        SS = (3, 3)
        MLP_HID = 4 * DIM
        N = WS[0] * WS[1]

        def _rel_pos_index():
            ch = np.arange(WS[0])
            cw = np.arange(WS[1])
            coords = np.stack(np.meshgrid(ch, cw, indexing='ij'))
            cf = coords.reshape(2, -1)
            rel = cf[:, :, None] - cf[:, None, :]
            rel = rel.transpose(1, 2, 0).copy()
            rel[:, :, 0] += WS[0] - 1
            rel[:, :, 1] += WS[1] - 1
            rel[:, :, 0] *= 2 * WS[1] - 1
            return rel.sum(-1)

        def _attn_mask(Hp, Wp):
            img = np.zeros((Hp, Wp), dtype=np.float32)
            cnt = 0
            hs = (slice(0, -WS[0]), slice(-WS[0], -SS[0]), slice(-SS[0], None))
            ws_ = (slice(0, -WS[1]), slice(-WS[1], -SS[1]), slice(-SS[1], None))
            for h in hs:
                for w in ws_:
                    img[h, w] = cnt
                    cnt += 1
            mw = img.reshape(Hp // WS[0], WS[0], Wp // WS[1], WS[1]).transpose(0, 2, 1, 3).reshape(-1, N)
            diff = mw[:, None, :] - mw[:, :, None]
            return np.where(diff != 0, -100.0, 0.0).astype(np.float32)

        def _ln(x, w, b):
            m = x.mean(-1, keepdims=True)
            v = ((x - m) ** 2).mean(-1, keepdims=True)
            return (x - m) * jax.lax.rsqrt(v + 1e-05) * w + b
        key = jax.random.key(seed)
        ks = jax.random.split(key, 16)
        d = DIM
        inp = {'x': jax.random.normal(ks[0], (16, 56, 56, d), jnp.float32), 'norm1_w': jnp.ones((d,), jnp.float32), 'norm1_b': jnp.zeros((d,), jnp.float32), 'qkv_w': jax.random.normal(ks[1], (d, 3 * d), jnp.float32) * 0.02, 'qkv_b': jnp.zeros((3 * d,), jnp.float32), 'rel_bias_table': jax.random.normal(ks[2], ((2 * WS[0] - 1) * (2 * WS[1] - 1), NH), jnp.float32) * 0.02, 'proj_w': jax.random.normal(ks[3], (d, d), jnp.float32) * 0.02, 'proj_b': jnp.zeros((d,), jnp.float32), 'norm2_w': jnp.ones((d,), jnp.float32), 'norm2_b': jnp.zeros((d,), jnp.float32), 'mlp_w1': jax.random.normal(ks[4], (d, MLP_HID), jnp.float32) * 0.02, 'mlp_b1': jnp.zeros((MLP_HID,), jnp.float32), 'mlp_w2': jax.random.normal(ks[5], (MLP_HID, d), jnp.float32) * 0.02, 'mlp_b2': jnp.zeros((d,), jnp.float32)}
        return inp
    _L1_conv_all = _L1_conv_setup()
    _L1_conv_in = {k: v for k, v in _L1_conv_all.items() if k in ('norm1_w', 'norm1_b', 'qkv_w', 'qkv_b', 'rel_bias_table', 'proj_w', 'proj_b', 'norm2_w', 'norm2_b', 'mlp_w1', 'mlp_b1', 'mlp_w2', 'mlp_b2')}
    del _L1_conv_all
    return {'x': x, 'L0_conv_ln1_g': _L0_conv_in['ln1_g'], 'L0_conv_ln1_b': _L0_conv_in['ln1_b'], 'L0_conv_qkv_w': _L0_conv_in['qkv_w'], 'L0_conv_qkv_b': _L0_conv_in['qkv_b'], 'L0_conv_proj_w': _L0_conv_in['proj_w'], 'L0_conv_proj_b': _L0_conv_in['proj_b'], 'L0_conv_rpb_table': _L0_conv_in['rpb_table'], 'L0_conv_ln2_g': _L0_conv_in['ln2_g'], 'L0_conv_ln2_b': _L0_conv_in['ln2_b'], 'L0_conv_fc1_w': _L0_conv_in['fc1_w'], 'L0_conv_fc1_b': _L0_conv_in['fc1_b'], 'L0_conv_ln3_g': _L0_conv_in['ln3_g'], 'L0_conv_ln3_b': _L0_conv_in['ln3_b'], 'L0_conv_fc2_w': _L0_conv_in['fc2_w'], 'L0_conv_fc2_b': _L0_conv_in['fc2_b'], 'L1_conv_norm1_w': _L1_conv_in['norm1_w'], 'L1_conv_norm1_b': _L1_conv_in['norm1_b'], 'L1_conv_qkv_w': _L1_conv_in['qkv_w'], 'L1_conv_qkv_b': _L1_conv_in['qkv_b'], 'L1_conv_rel_bias_table': _L1_conv_in['rel_bias_table'], 'L1_conv_proj_w': _L1_conv_in['proj_w'], 'L1_conv_proj_b': _L1_conv_in['proj_b'], 'L1_conv_norm2_w': _L1_conv_in['norm2_w'], 'L1_conv_norm2_b': _L1_conv_in['norm2_b'], 'L1_conv_mlp_w1': _L1_conv_in['mlp_w1'], 'L1_conv_mlp_b1': _L1_conv_in['mlp_b1'], 'L1_conv_mlp_w2': _L1_conv_in['mlp_w2'], 'L1_conv_mlp_b2': _L1_conv_in['mlp_b2']}

def reference(x, L0_conv_ln1_g, L0_conv_ln1_b, L0_conv_qkv_w, L0_conv_qkv_b, L0_conv_proj_w, L0_conv_proj_b, L0_conv_rpb_table, L0_conv_ln2_g, L0_conv_ln2_b, L0_conv_fc1_w, L0_conv_fc1_b, L0_conv_ln3_g, L0_conv_ln3_b, L0_conv_fc2_w, L0_conv_fc2_b, L1_conv_norm1_w, L1_conv_norm1_b, L1_conv_qkv_w, L1_conv_qkv_b, L1_conv_rel_bias_table, L1_conv_proj_w, L1_conv_proj_b, L1_conv_norm2_w, L1_conv_norm2_b, L1_conv_mlp_w1, L1_conv_mlp_b1, L1_conv_mlp_w2, L1_conv_mlp_b2):
    import jax
    import jax.numpy as jnp

    def _L0_conv_ref(x, ln1_g, ln1_b, qkv_w, qkv_b, proj_w, proj_b, rpb_table, ln2_g, ln2_b, fc1_w, fc1_b, ln3_g, ln3_b, fc2_w, fc2_b):
        import jax, jax.numpy as jnp
        import numpy as np
        WS = 7
        SS = 3
        NH = 4
        EPS = 1e-05

        def _rel_pos_index(ws):
            coords = np.stack(np.meshgrid(np.arange(ws), np.arange(ws), indexing='ij')).reshape(2, -1)
            rel = coords[:, :, None] - coords[:, None, :]
            rel = rel.transpose(1, 2, 0).astype(np.int64)
            rel[..., 0] += ws - 1
            rel[..., 1] += ws - 1
            rel[..., 0] *= 2 * ws - 1
            return rel.sum(-1)

        def _shift_mask(H, W, ws, ss):
            img = np.zeros((H, W), dtype=np.float32)
            cnt = 0
            for h in (slice(0, -ws), slice(-ws, -ss), slice(-ss, None)):
                for w in (slice(0, -ws), slice(-ws, -ss), slice(-ss, None)):
                    img[h, w] = cnt
                    cnt += 1
            mw = img.reshape(H // ws, ws, W // ws, ws).transpose(0, 2, 1, 3).reshape(-1, ws * ws)
            diff = mw[:, None, :] - mw[:, :, None]
            return np.where(diff != 0, -100.0, 0.0).astype(np.float32)

        def _ln(x, g, b):
            m = jnp.mean(x, axis=-1, keepdims=True)
            v = jnp.mean(jnp.square(x - m), axis=-1, keepdims=True)
            return (x - m) * jax.lax.rsqrt(v + EPS) * g + b
        B, H, W, C = x.shape
        N = WS * WS
        hd = C // NH
        scale = hd ** (-0.5)
        nW = H // WS * (W // WS)
        rpi = jnp.asarray(_rel_pos_index(WS))
        rel_bias = rpb_table[rpi.reshape(-1)].reshape(N, N, NH)
        rel_bias = jnp.transpose(rel_bias, (2, 0, 1))
        attn_mask = jnp.asarray(_shift_mask(H, W, WS, SS))
        h = _ln(x, ln1_g, ln1_b)
        h = jnp.roll(h, (-SS, -SS), axis=(1, 2))
        h = h.reshape(B, H // WS, WS, W // WS, WS, C)
        h = jnp.transpose(h, (0, 1, 3, 2, 4, 5)).reshape(B * nW, N, C)
        qkv = h @ qkv_w + qkv_b
        qkv = qkv.reshape(B * nW, N, 3, NH, hd)
        q, k, v = (qkv[:, :, 0], qkv[:, :, 1], qkv[:, :, 2])
        attn = jnp.einsum('wqhd,wkhd->whqk', q * scale, k)
        attn = attn + rel_bias[None]
        attn = attn.reshape(B, nW, NH, N, N) + attn_mask[None, :, None]
        attn = jax.nn.softmax(attn.reshape(B * nW, NH, N, N), axis=-1)
        o = jnp.einsum('whqk,wkhd->wqhd', attn, v).reshape(B * nW, N, C)
        o = o @ proj_w + proj_b
        o = o.reshape(B, H // WS, W // WS, WS, WS, C)
        o = jnp.transpose(o, (0, 1, 3, 2, 4, 5)).reshape(B, H, W, C)
        o = jnp.roll(o, (SS, SS), axis=(1, 2))
        x = x + o
        m = _ln(x, ln2_g, ln2_b)
        m = jax.nn.gelu(m @ fc1_w + fc1_b, approximate=False)
        m = _ln(m, ln3_g, ln3_b)
        m = m @ fc2_w + fc2_b
        return x + m

    def _L1_conv_ref(x, norm1_w, norm1_b, qkv_w, qkv_b, rel_bias_table, proj_w, proj_b, norm2_w, norm2_b, mlp_w1, mlp_b1, mlp_w2, mlp_b2):
        import jax, jax.numpy as jnp
        import numpy as np
        DIM = 96
        NH = 12
        WS = (7, 7)
        SS = (3, 3)
        MLP_HID = 4 * DIM
        N = WS[0] * WS[1]

        def _rel_pos_index():
            ch = np.arange(WS[0])
            cw = np.arange(WS[1])
            coords = np.stack(np.meshgrid(ch, cw, indexing='ij'))
            cf = coords.reshape(2, -1)
            rel = cf[:, :, None] - cf[:, None, :]
            rel = rel.transpose(1, 2, 0).copy()
            rel[:, :, 0] += WS[0] - 1
            rel[:, :, 1] += WS[1] - 1
            rel[:, :, 0] *= 2 * WS[1] - 1
            return rel.sum(-1)

        def _attn_mask(Hp, Wp):
            img = np.zeros((Hp, Wp), dtype=np.float32)
            cnt = 0
            hs = (slice(0, -WS[0]), slice(-WS[0], -SS[0]), slice(-SS[0], None))
            ws_ = (slice(0, -WS[1]), slice(-WS[1], -SS[1]), slice(-SS[1], None))
            for h in hs:
                for w in ws_:
                    img[h, w] = cnt
                    cnt += 1
            mw = img.reshape(Hp // WS[0], WS[0], Wp // WS[1], WS[1]).transpose(0, 2, 1, 3).reshape(-1, N)
            diff = mw[:, None, :] - mw[:, :, None]
            return np.where(diff != 0, -100.0, 0.0).astype(np.float32)

        def _ln(x, w, b):
            m = x.mean(-1, keepdims=True)
            v = ((x - m) ** 2).mean(-1, keepdims=True)
            return (x - m) * jax.lax.rsqrt(v + 1e-05) * w + b
        B, H, W, C = x.shape
        hd = C // NH
        scale = hd ** (-0.5)
        shortcut = x
        xn = _ln(x, norm1_w, norm1_b)
        sx = jnp.roll(xn, (-SS[0], -SS[1]), axis=(1, 2))
        nWh, nWw = (H // WS[0], W // WS[1])
        nW = nWh * nWw
        xw = sx.reshape(B, nWh, WS[0], nWw, WS[1], C).transpose(0, 1, 3, 2, 4, 5).reshape(B * nW, N, C)
        qkv = (xw @ qkv_w + qkv_b).reshape(B * nW, N, 3, NH, hd).transpose(2, 0, 3, 1, 4)
        q, k, v = (qkv[0] * scale, qkv[1], qkv[2])
        attn = jnp.einsum('whnd,whmd->whnm', q, k)
        rpi = _rel_pos_index().reshape(-1)
        bias = rel_bias_table[rpi].reshape(N, N, NH).transpose(2, 0, 1)
        attn = attn + bias[None]
        mask = jnp.asarray(_attn_mask(H, W))
        attn = attn.reshape(B, nW, NH, N, N) + mask[None, :, None]
        attn = jax.nn.softmax(attn.reshape(B * nW, NH, N, N), axis=-1)
        out = jnp.einsum('whnm,whmd->whnd', attn, v).transpose(0, 2, 1, 3).reshape(B * nW, N, C)
        out = out @ proj_w + proj_b
        sx = out.reshape(B, nWh, nWw, WS[0], WS[1], C).transpose(0, 1, 3, 2, 4, 5).reshape(B, H, W, C)
        x = jnp.roll(sx, (SS[0], SS[1]), axis=(1, 2))
        x = shortcut + x
        h = _ln(x, norm2_w, norm2_b)
        h = jax.nn.gelu(h @ mlp_w1 + mlp_b1, approximate=False) @ mlp_w2 + mlp_b2
        return x + h

    def _gn(v, G=32, eps=1e-05):
        B_, H_, W_, C_ = v.shape
        g = v.reshape(B_, H_, W_, G, C_ // G)
        m = jnp.mean(g, axis=(1, 2, 4), keepdims=True)
        s = jnp.var(g, axis=(1, 2, 4), keepdims=True)
        return ((g - m) / jnp.sqrt(s + eps)).reshape(v.shape)

    def _ln_c(v, eps=1e-06):
        m = jnp.mean(v, axis=-1, keepdims=True)
        s = jnp.var(v, axis=-1, keepdims=True)
        return (v - m) / jnp.sqrt(s + eps)

    def _ln_t(v, eps=1e-05):
        m = jnp.mean(v, axis=-1, keepdims=True)
        s = jnp.var(v, axis=-1, keepdims=True)
        return (v - m) / jnp.sqrt(s + eps)

    def _to_tokens(v):
        B_, H_, W_, C_ = v.shape
        return v.reshape(B_, H_ * W_, C_)

    def _from_tokens(t, like):
        return t.reshape(like.shape)
    x = _L0_conv_ref(x, L0_conv_ln1_g, L0_conv_ln1_b, L0_conv_qkv_w, L0_conv_qkv_b, L0_conv_proj_w, L0_conv_proj_b, L0_conv_rpb_table, L0_conv_ln2_g, L0_conv_ln2_b, L0_conv_fc1_w, L0_conv_fc1_b, L0_conv_ln3_g, L0_conv_ln3_b, L0_conv_fc2_w, L0_conv_fc2_b)
    x = _L1_conv_ref(x, L1_conv_norm1_w, L1_conv_norm1_b, L1_conv_qkv_w, L1_conv_qkv_b, L1_conv_rel_bias_table, L1_conv_proj_w, L1_conv_proj_b, L1_conv_norm2_w, L1_conv_norm2_b, L1_conv_mlp_w1, L1_conv_mlp_b1, L1_conv_mlp_w2, L1_conv_mlp_b2)
    return x

_drawn_inputs = setup_inputs


def setup_inputs(seed=0):
    import zlib

    import numpy as np

    out = dict(_drawn_inputs(seed))
    spreads = {'L0_conv_ln1_g': (1.0, 0.6),
     'L0_conv_ln1_b': (0.0, 0.8),
     'L0_conv_qkv_b': (0.0, 0.474),
     'L0_conv_proj_b': (0.0, 0.1),
     'L0_conv_ln2_g': (1.0, 0.2),
     'L0_conv_ln2_b': (0.0, 0.28),
     'L0_conv_fc1_b': (0.0, 0.1),
     'L0_conv_ln3_g': (1.0, 0.2),
     'L0_conv_ln3_b': (0.0, 0.358),
     'L0_conv_fc2_b': (0.0, 0.1),
     'L1_conv_norm1_w': (1.0, 0.6),
     'L1_conv_norm1_b': (0.0, 0.8),
     'L1_conv_qkv_b': (0.0, 0.451),
     'L1_conv_proj_b': (0.0, 0.1),
     'L1_conv_norm2_w': (1.0, 0.6),
     'L1_conv_norm2_b': (0.0, 2.0),
     'L1_conv_mlp_b1': (0.0, 0.404),
     'L1_conv_mlp_b2': (0.0, 0.1)}
    factors = {'L0_conv_qkv_w': 7.857,
     'L0_conv_proj_w': 3.079,
     'L0_conv_rpb_table': 8.0,
     'L1_conv_qkv_w': 5.206,
     'L1_conv_rel_bias_table': 25.721,
     'L1_conv_proj_w': 2.74}
    for name, (base, spread) in spreads.items():
        noise = np.random.default_rng([zlib.crc32(name.encode()), seed]).standard_normal(out[name].shape)
        drawn = base * np.exp(spread * noise) if base else spread * noise
        out[name] = jnp.asarray(drawn.astype(out[name].dtype))
    for name, factor in factors.items():
        out[name] = (out[name] * factor).astype(out[name].dtype)
    return out
```

```python
import concourse.bass as bass
from concourse import mybir
from contextlib import ExitStack
import numpy as np

NSTRIP, ROWS_IN_IMAGE = 256, 8
WS, SHIFT = 7, 3
TOK = WS * WS
HALF = (0, 64)
SP = 64 + TOK
PAIRS = 4
PT = 2 * TOK
ST = PAIRS * PT
C, HID, HCH = 96, 384, 3
NH = (4, 12)
HD = (C // NH[0], C // NH[1])
UNITS = (NH[0] // 4 * 2, NH[1] // 4 * 2)
NHP = (NH[0] // 2, NH[1] // 2)
TCH = C // 2
VW = tuple(TCH + n // 2 for n in NH)
OROWS = 64 + max(VW)
EPS = 1e-5
NREG = 6
BK = 2 * TOK + NREG


def _regions():
    r = (np.arange(WS) >= WS - SHIFT).astype(int)
    return np.repeat(r, WS), np.tile(r, WS)


def shape_constants():
    rr, rc = _regions()
    k = {}
    k["ident"] = np.eye(128, dtype=np.float32)
    c = np.arange(C)
    k["kmask"] = np.stack([(c // HD[0])[:, None] == np.arange(4), (c % 32 // HD[1])[:, None] == np.arange(4)], 1)\
        .reshape(C, 8).astype(np.float32)
    rep = (np.arange(PT) // TOK)[:, None]
    k["vmask"] = np.concatenate([(np.arange(2 * HD[L]) // HD[L])[None] == rep for L in (0, 1)], 1).astype(np.float32)
    for L in (0, 1):
        v = np.zeros((PT, 8, NHP[L], VW[L]), np.float32)
        for hp in range(NHP[L]):
            local = hp % (NHP[L] // 2)
            for r in (0, 1):
                v[r * TOK:(r + 1) * TOK, :, hp, TCH + 2 * local + r] = 1
        k[f"vinit{L}"] = v.reshape(PT, -1)
        e = np.zeros((OROWS, OROWS), np.float32)
        for r in range(OROWS):
            t, cc = divmod(r, 64)
            if cc < TCH:
                e[64 * t + TCH + cc // HD[L], r] = 1
            elif cc < VW[L]:
                e[r, r] = 1
            else:
                e[TCH, r] = 1
        k[f"spread{L}"] = e
    left = np.zeros((BK, 2, SP), np.float32)
    for part in (0, 1):
        for h in HALF:
            left[part * TOK + np.arange(TOK), :, h + np.arange(TOK)] = 1
    for q in range(TOK):
        left[2 * TOK + rr[q], :, HALF[0] + q] = 1
        left[2 * TOK + rr[q], 0, HALF[1] + q] = 1
        left[2 * TOK + 2 + 2 * rr[q] + rc[q], 1, HALF[1] + q] = 1
    k["tleft"] = left.reshape(BK, -1)
    right = np.zeros((NREG, 2, sum(NH), TOK), np.float32)
    for g in (0, 1):
        right[g, 1] = -100.0 * (rr != g)
        for h in (0, 1):
            right[2 + 2 * g + h, 0] = -100.0 * (rc != h)
            right[2 + 2 * g + h, 1] = -100.0 * ((rr != g) | (rc != h))
    k["tmask"] = right.reshape(NREG, -1)
    k["tlow"] = -(np.arange(BK) // TOK == 1).astype(np.float32)[:, None]
    return k


class Strip:

    def __init__(self, i, off):
        self.i, self.off = i, off
        self.known = isinstance(i, int)

    def back(self, n=1):
        return Strip(self.i, self.off + n)

    def exists(self, n):
        return not self.known or 0 <= self.i - self.off < n

    def count(self, per, c):
        return (self.i - self.off) * per + c if self.known else self.i * per + (c - self.off * per)


def swin_program(nc, d, out, ns=NSTRIP, last_row_from=NSTRIP - NSTRIP // ROWS_IN_IMAGE):
    f32, f32r = mybir.dt.float32, mybir.dt.float32r
    ALU, ACT, AX = mybir.AluOpType, mybir.ActivationFunctionType, mybir.AxisListType
    assert (last_row_from + 256) >= 0
    ctx = ExitStack()
    with ctx:
        def sb(name, shape, dt=f32):
            return ctx.enter_context(nc.sbuf_tensor(name, shape, dt))

        def bank(name, shape=(128, 512)):
            return ctx.enter_context(nc.psum_tensor(name, list(shape), f32))

        def sem(name):
            return ctx.enter_context(nc.semaphore(name))

        def free(ap, *dims):
            return bass.AP(ap.tensor, ap.offset, [list(ap.ap[0])] + [list(x) for x in dims])

        ident = sb("ident", [128, 128])
        kmask = sb("kmask", [C, 8])
        vmask = sb("vmask", [PT, 2 * HD[0] + 2 * HD[1]])
        spread = [sb(f"spread{L}", [OROWS, OROWS]) for L in (0, 1)]
        tleft_in = sb("tleft_in", [BK, 2 * SP])
        tlow = sb("tlow", [BK, 1])
        NT = TOK * sum(NH)
        t_in = sb("t_in", [BK, 2 * NT])
        t_high = sb("t_high", [BK, 2 * NT], f32r)
        tleft = sb("tleft", [BK, 2 * SP], f32r)
        table = sb("table", [BK, 2 * NT], f32r)
        NP96 = 7 + 3 * C + HID + C
        par96 = [sb(f"par96_{L}", [C, NP96]) for L in (0, 1)]
        NP128 = 9 + HCH * C
        par128 = [sb(f"par128_{L}", [128, NP128]) for L in (0, 1)]
        rows = [sb(f"rows{L}", [1, 2 * C]) for L in (0, 1)]
        wqkv = [sb(f"wqkv{L}", [C, 3 * C]) for L in (0, 1)]
        bqkv = [sb(f"bqkv{L}", [C, 3]) for L in (0, 1)]
        wproj = [sb(f"wproj{L}", [OROWS, C]) for L in (0, 1)]
        brow = [sb(f"brow{L}", [1, C]) for L in (0, 1)]
        wfc1 = [sb(f"wfc1_{L}", [C, HID]) for L in (0, 1)]
        bfc1 = [sb(f"bfc1_{L}", [128, HCH]) for L in (0, 1)]
        wg3 = sb("wg3", [128, HCH * C])
        wfc2 = sb("wfc2", [128, HCH, C + 1])
        ones = sb("ones", [128, 128])
        mean_w = sb("mean_w", [128, 128])
        bfc2 = [sb(f"bfc2_{L}", [PT, C]) for L in (0, 1)]

        x_in = sb("x_in", [PT, PAIRS, C])
        x_mid0 = sb("x_mid0", [PT, PAIRS, C])
        x_next = sb("x_next", [PT, PAIRS, C])
        x_keep = sb("x_keep", [PT, PAIRS, C])
        x_mid1 = sb("x_mid1", [PT, PAIRS, C])
        x_biased = [sb(f"x_biased{L}", [PT, PAIRS, C]) for L in (0, 1)]
        y_out = sb("y_out", [PT, PAIRS, C])
        LN = ("A0", "M0", "A1", "M1")
        bn = {n: sb("bn" + n, [PT, PAIRS, 6]) for n in LN}
        mv = {n: sb("mv" + n, [PT, PAIRS, 2]) for n in LN}
        var_eps = {n: sb("var_eps" + n, [PT, PAIRS]) for n in LN}
        gate = sb("gate", [1, 1])
        minus_half = sb("minus_half", [PT, PAIRS])
        rstd = {n: sb("rstd" + n, [PT, PAIRS]) for n in LN}
        xn = {n: sb("xn" + n, [PT, PAIRS, C]) for n in LN}
        xnT_a = sb("xnT_a", [C, 8, 2, TOK])
        xnT_m = sb("xnT_m", [C, ST])
        qT = [sb(f"qT{L}", [C, ST]) for L in (0, 1)]
        kT = sb("kT", [C, ST])
        kM = [sb(f"kM{L}", [C, 4, ST]) for L in (0, 1)]
        vM = [sb(f"vM{L}", [PT, 8, NHP[L], VW[L]]) for L in (0, 1)]
        negmax = [sb(f"negmax{n}", [SP, 8]) for n in (0, 1)]
        shifted = [sb(f"shifted{n}", [SP, 2 * 4 * TOK]) for n in (0, 1)]
        probs = [sb(f"probs{n}", [SP, 2 * 4 * TOK]) for n in (0, 1)]
        probsT = [sb(f"probsT{n}", [PT, 4, 2, TOK]) for n in (0, 1)]
        o_raw = sb("o_raw", [OROWS, ST])
        o_rden = sb("o_rden", [OROWS, ST])
        o_norm = sb("o_norm", [OROWS, ST])
        hid = sb("hid", [128, HCH, ST])
        hid_sq = sb("hid_sq", [128, HCH, ST])
        hid_ss = sb("hid_ss", [128, ST])
        st3 = sb("st3", [PT, PAIRS, 2])
        var3 = sb("var3", [PT, PAIRS])
        rstd3 = sb("rstd3", [PT, PAIRS])

        ps_s = [bank(f"ps_s{n}") for n in range(2)]
        ps_t = [bank(f"ps_t{n}") for n in range(2)]
        ps_o = bank("ps_o")
        ps_g = [bank(f"ps_g{n}") for n in range(3)]

        s_const = sem("s_const")
        s_memset = sem("s_memset")
        s_w = sem("s_w")
        s_wps = sem("s_wps")
        s_brow = sem("s_brow")
        s_load = sem("s_load")
        s_store = sem("s_store")
        s_bn = {n: sem("s_bn" + n) for n in LN}
        s_var = {n: sem("s_var" + n) for n in LN}
        s_rstd = {n: sem("s_rstd" + n) for n in LN}
        s_xn = {n: sem("s_xn" + n) for n in LN}
        s_xt = {n: sem("s_xt" + n) for n in LN}
        s_xe = {n: sem("s_xe" + n) for n in LN}
        pairsem = lambda name: [sem(f"{name}{L}") for L in (0, 1)]
        s_q, s_qe = pairsem("s_q"), pairsem("s_qe")
        s_k, s_ke = pairsem("s_k"), pairsem("s_ke")
        s_km = pairsem("s_km")
        s_v, s_vm = pairsem("s_v"), pairsem("s_vm")
        s_s = pairsem("s_s")
        s_mx = pairsem("s_mx")
        s_sh = pairsem("s_sh")
        s_ex = pairsem("s_ex")
        s_pt, s_pe = pairsem("s_pt"), pairsem("s_pe")
        s_pv = pairsem("s_pv")
        s_oe = pairsem("s_oe")
        s_sp = pairsem("s_sp")
        s_rd = pairsem("s_rd")
        s_on = pairsem("s_on")
        s_pj = pairsem("s_pj")
        s_xo = pairsem("s_xo")
        s_xb = pairsem("s_xb")
        s_f1, s_ge = pairsem("s_f1"), pairsem("s_ge")
        s_sq = sem("s_sq")
        s_f2 = pairsem("s_f2")
        s_v3 = sem("s_v3")
        s_rstd3 = sem("s_rstd3")
        s_fin = pairsem("s_fin")
        s_keep = sem("s_keep")

        def user_before(i, users, slots, at):
            p, lag = at - 1, 0
            for _ in range(4 * len(users)):
                if p < 0:
                    p, lag = p + len(users), lag + 1
                semaphore, off, per, c = users[p]
                if slots[p] == slots[at] and Strip(i, off + lag).exists(ns):
                    return semaphore, Strip(i, off + lag).count(per, c)
                p -= 1
            return None

        LAG = {"A0": 0, "M0": 1, "A1": 2, "M1": 3}
        ULAG = (1, 2)
        MLAG = (1, 3)

        G = ["xtA1", "q1", "k1", "va1", "vb1", "xtM1", "f1_0_1", "f1_1_1", "f1_2_1", "sp0", "f2_1", "pj0",
             "xtM0", "f1_0_0", "f1_1_0", "f1_2_0", "xtA0", "q0", "k0", "sp1", "f2_0", "va0", "vb0", "pj1"]
        free_by = {}
        for n in LN:
            free_by["xt" + n] = (s_xe[n], LAG[n], 1, 1)
        for L in (0, 1):
            a = LAG[f"A{L}"]
            free_by[f"q{L}"] = (s_qe[L], a, 1, 1)
            free_by[f"k{L}"] = (s_ke[L], a, 1, 1)
            free_by[f"va{L}"] = (s_vm[L], a, 2, 1)
            free_by[f"vb{L}"] = (s_vm[L], a, 2, 2)
            free_by[f"sp{L}"] = (s_rd[L], ULAG[L], 1, 1)
            free_by[f"pj{L}"] = (s_xo[L], ULAG[L], 1, 1)
            for c in range(HCH):
                free_by[f"f1_{c}_{L}"] = (s_ge[L], MLAG[L], HCH, c + 1)
            free_by[f"f2_{L}"] = (s_fin[L], MLAG[L], 1, 1)
        g_users = [free_by[n] for n in G]
        g_slots = [n % 3 for n in range(len(G))]

        def g_bank(i, name):
            at = G.index(name)
            return ps_g[at % 3], user_before(i, g_users, g_slots, at)

        units = [(L, u) for L in (0, 1) for u in range(UNITS[L])]
        by_unit = lambda s: [(s[L], ULAG[L], UNITS[L], u + 1) for L, u in units]
        two = [n % 2 for n in range(len(units))]

        def unit_place(L, u):
            return u // (UNITS[L] // 2), u % (UNITS[L] // 2), units.index((L, u))

        NCONST = 0
        loads = [(ident[:, :], d["ident"]), (kmask[:, :], d["kmask"]), (vmask[:, :], d["vmask"]),
                 (tleft_in[:, :], d["tleft"]), (tlow[:, :], d["tlow"]),
                 (t_in[2 * TOK:BK, :], d["tmask"])]
        for v in (0, 1):
            loads.append((t_in[0:2 * TOK, v * NT:(v + 1) * NT], d["tab"]))
        for L in (0, 1):
            loads += [(spread[L][:, :], d[f"spread{L}"]), (par96[L][:, :], d[f"par96_{L}"]),
                      (par128[L][:, :], d[f"par128_{L}"]), (rows[L][:, :], d[f"rows{L}"]),
                      (wproj[L][:, :], d[f"wproj{L}"]),
                      (vM[L][:, :, :, :].rearrange("p w h c -> p (w h c)"), d[f"vinit{L}"])]
        NCONST = 16 * len(loads)
        P96 = {"g1": 0, "b1": 1, "bqkv": 2, "g2": 5, "b2": 6, "qkv": 7, "fc1": 7 + 3 * C, "proj": 7 + 3 * C + HID}
        P128 = {"g3": 0, "b3": 3, "bfc1": 6, "fc2": 9}

        def iterate(eng, body):
            total, first = ns + 3, 4
            for i in range(min(first, total)):
                body(i)
            if ns > first:
                with eng.Fori(first, ns) as i:
                    body(i)
            for i in range(max(first, ns), total):
                body(i)

        block = ctx.enter_context(nc.Block())

        @block.sync
        def _(sp):
            for dst, src in loads:
                sp.dma_start(dst, src).then_inc(s_const, 16)
            for L in (0, 1):
                sp.wait_ge(s_w, 10 + L)
                sp.dma_start(wproj[L][TCH:TCH + 1, :], brow[L][0:1, :]).then_inc(s_brow, 16)

            def body(i):
                a0 = Strip(i, 0)
                if a0.exists(ns):
                    if a0.back().exists(ns):
                        sp.wait_ge(s_xo[0], a0.back().count(1, 1))
                    n = i if isinstance(i, int) else bass.ds(i, 1)
                    src = d["x"][n, :, :] if isinstance(i, int) else d["x"][n, :, :].rearrange("a p c -> (a p) c")
                    sp.dma_start(x_in[:, :, :].rearrange("p a c -> p (a c)"), src).then_inc(s_load, 16)
                m1 = Strip(i, 3)
                if m1.exists(ns):
                    sp.wait_ge(s_fin[1], m1.count(1, 1))
                    if isinstance(i, int):
                        dst = out[i - 3, :, :]
                    else:
                        dst = out[bass.ds(i - 3, 1), :, :].rearrange("a p c -> (a p) c")
                    sp.dma_start(dst, y_out[:, :, :].rearrange("p a c -> p (a c)")).then_inc(s_store, 16)

            iterate(sp, body)
            sp.wait_ge(s_store, 16 * ns)

        @block.tensor
        def _(pe):
            pe.wait_ge(s_const, NCONST)
            pe.wait_ge(s_memset, 4)
            for L in (0, 1):
                p = par96[L]
                for n in range(3):
                    pe.matmul(ps_g[L][0:C, n:n + 1], p[:, P96["qkv"] + C * n:P96["qkv"] + C * (n + 1)],
                              p[:, P96["b1"]:P96["b1"] + 1], start=True, stop=True)
                for n in range(HCH):
                    mm = pe.matmul(ps_g[L][:, 3 + n:4 + n], p[:, P96["fc1"] + 128 * n:P96["fc1"] + 128 * (n + 1)],
                                   p[:, P96["b2"]:P96["b2"] + 1], start=True, stop=True)
                mm.then_inc(s_wps, 1)
            for L in (0, 1):
                pe.wait_ge(s_w, 2 + 2 * L)
                pe.matmul(ps_s[L][0:1, 0:C], bqkv[L][:, 2:3], par96[L][:, P96["proj"]:P96["proj"] + C],
                          start=True, stop=True).then_inc(s_wps, 1)
            pe.wait_ge(s_w, 6)
            for c in range(HCH):
                mm = pe.matmul(ps_g[2][:, 0:C], mean_w[:, :], wg3[:, C * c:C * (c + 1)], start=(c == 0), stop=(c == HCH - 1))
            mm.then_inc(s_wps, 1)
            pe.wait_ge(s_w, 7)
            for c in range(HCH):
                pe.matmul(ps_t[0][0:PT, 0:C], hid_sq[:, c, 0:PT], par128[0][:, P128["fc2"] + C * c:P128["fc2"] + C * (c + 1)],
                          start=(c == 0), stop=False)
            pe.matmul(ps_t[0][0:PT, 0:C], ones[0:1, 0:PT], rows[0][0:1, C:2 * C], start=False, stop=True)
            pe.matmul(ps_t[1][0:PT, 0:C], ones[0:1, 0:PT], rows[1][0:1, C:2 * C], start=True, stop=True).then_inc(s_wps, 1)
            pe.wait_ge(s_w, 15)
            pe.wait_ge(s_brow, 32)

            def xT(i, n):
                x = Strip(i, LAG[n])
                if x.exists(ns):
                    pe.wait_ge(s_xn[n], x.count(1, 1))
                    g, before = g_bank(i, "xt" + n)
                    if before:
                        pe.wait_ge(*before)
                    for p in range(PAIRS):
                        mm = pe.transpose(g[0:C, p * PT:(p + 1) * PT], xn[n][:, p, :], ident[0:PT, 0:PT])
                    mm.then_inc(s_xt[n], 1)

            def qk(i, L, name, part, signal):
                x = Strip(i, LAG[f"A{L}"])
                if x.exists(ns):
                    pe.wait_ge(s_xe[f"A{L}"], x.count(1, 1))
                    g, before = g_bank(i, f"{name}{L}")
                    if before:
                        pe.wait_ge(*before)
                    pe.matmul(g[0:C, 0:ST], wqkv[L][:, part * C:(part + 1) * C], xnT_a[:, :, 0, :], start=True, stop=True)\
                      .then_inc(signal[L], 1)

            def v(i, L, half):
                x = Strip(i, LAG[f"A{L}"])
                if x.exists(ns):
                    pe.wait_ge(s_xe[f"A{L}"], x.count(1, 1))
                    g, before = g_bank(i, ("va", "vb")[half] + str(L))
                    if before:
                        pe.wait_ge(*before)
                    for n in range(4):
                        w = 4 * half + n
                        twice = xnT_a[:, w, :, :].rearrange("p r t -> p (r t)")
                        mm = pe.matmul(g[0:PT, n * C:(n + 1) * C], twice, wqkv[L][:, 2 * C:3 * C], start=True, stop=True)
                    mm.then_inc(s_v[L], 1)

            def scores(i, L, u):
                x = Strip(i, ULAG[L])
                if not x.exists(ns):
                    return
                two_pairs, group, at = unit_place(L, u)
                if before := user_before(i, by_unit(s_sh), two, at):
                    pe.wait_ge(*before)
                s = ps_s[at % 2]
                pe.wait_ge(s_qe[L], x.count(1, 1))
                pe.wait_ge(s_km[L], x.count(1, 1))
                col = TOK * (4 * group + (NH[0] if L else 0))
                if x.known:
                    start = (1 if i - ULAG[L] >= last_row_from else 0) * NT + col
                    tab = table[:, start:start + 4 * TOK]
                else:
                    which = (i + (256 - last_row_from - ULAG[L])) // 256
                    tab = table[:, bass.ds(which * NT + col, 4 * TOK)]
                for p in (0, 1):
                    left = 1 if 2 * two_pairs + p == PAIRS - 1 else 0
                    pe.matmul(s[0:SP, 4 * TOK * p:4 * TOK * (p + 1)], tleft[:, left * SP:(left + 1) * SP], tab,
                              start=(p == 0), stop=False, skip_group_check=True)
                r = slice(0, C) if L == 0 else slice(32 * group, 32 * group + 32)
                for p in (0, 1):
                    for h in (0, 1):
                        t = (2 * two_pairs + p) * PT + h * TOK
                        mm = pe.matmul(s[HALF[h]:HALF[h] + TOK, 4 * TOK * p:4 * TOK * (p + 1)], qT[L][r, t:t + TOK],
                                       kM[L][r, :, t:t + TOK], start=False, stop=True, skip_group_check=True)
                mm.then_inc(s_s[L], 1)

            def probs_turn(i, L, u):
                x = Strip(i, ULAG[L])
                if not x.exists(ns):
                    return
                _, _, at = unit_place(L, u)
                pe.wait_ge(s_ex[L], x.count(UNITS[L], u + 1))
                if before := user_before(i, by_unit(s_pe), two, at):
                    pe.wait_ge(*before)
                for n in range(4):
                    mm = pe.transpose(ps_t[at % 2][0:PT, n * SP:(n + 1) * SP], probs[at % 2][:, n * PT:(n + 1) * PT],
                                      ident[0:SP, 0:SP])
                mm.then_inc(s_pt[L], 1)

            def attend(i, L, u):
                x = Strip(i, ULAG[L])
                if not x.exists(ns):
                    return
                two_pairs, group, at = unit_place(L, u)
                pe.wait_ge(s_pe[L], x.count(UNITS[L], u + 1))
                pe.wait_ge(s_vm[L], x.count(2, 2))
                if u == 0:
                    if before := user_before(i, [(s_oe[0], ULAG[0], 1, 1), (s_oe[1], ULAG[1], 1, 1)], [0, 0], L):
                        pe.wait_ge(*before)
                begun = set()
                for p in (0, 1):
                    for h in (0, 1):
                        w = 2 * (2 * two_pairs + p) + h
                        for n in (0, 1):
                            hp = 2 * group + n
                            tile = hp // (NHP[L] // 2)
                            first = u == {(0, 0): 0, (0, 1): 0, (1, 0): 0, (1, 1): 1}[L, tile] and tile not in begun
                            begun.add(tile)
                            mm = pe.matmul(ps_o[64 * tile:64 * tile + VW[L], w * TOK:(w + 1) * TOK], vM[L][:, w, hp, :],
                                           probsT[at % 2][:, 2 * p + n, h, :], start=first, stop=True, skip_group_check=True)
                mm.then_inc(s_pv[L], 1)

            def spread_den(i, L):
                x = Strip(i, ULAG[L])
                if x.exists(ns):
                    pe.wait_ge(s_oe[L], x.count(1, 1))
                    g, before = g_bank(i, f"sp{L}")
                    if before:
                        pe.wait_ge(*before)
                    pe.matmul(g[0:OROWS, 0:ST], spread[L][:, :], o_raw[:, :], start=True, stop=True).then_inc(s_sp[L], 1)

            def project(i, L):
                x = Strip(i, ULAG[L])
                if x.exists(ns):
                    pe.wait_ge(s_on[L], x.count(1, 1))
                    g, before = g_bank(i, f"pj{L}")
                    if before:
                        pe.wait_ge(*before)
                    for p in range(PAIRS):
                        mm = pe.matmul(g[0:PT, p * C:(p + 1) * C], o_norm[:, p * PT:(p + 1) * PT], wproj[L][:, :],
                                       start=True, stop=True)
                    mm.then_inc(s_pj[L], 1)

            def fc1(i, L, c):
                x = Strip(i, MLAG[L])
                if x.exists(ns):
                    pe.wait_ge(s_xe[f"M{L}"], x.count(1, 1))
                    g, before = g_bank(i, f"f1_{c}_{L}")
                    if before:
                        pe.wait_ge(*before)
                    pe.matmul(g[:, 0:ST], wfc1[L][:, 128 * c:128 * (c + 1)], xnT_m[:, :], start=True, stop=True)\
                      .then_inc(s_f1[L], 1)

            def fc2(i, L):
                x = Strip(i, MLAG[L])
                if not x.exists(ns):
                    return
                pe.wait_ge(s_ge[L], x.count(HCH, HCH))
                if L == 0:
                    pe.wait_ge(s_sq, x.count(3, 3))
                g, before = g_bank(i, f"f2_{L}")
                if before:
                    pe.wait_ge(*before)
                step, width = (C + 2, C + 1) if L == 0 else (C, C)
                for p in range(PAIRS):
                    t = slice(p * PT, (p + 1) * PT)
                    for c in range(HCH):
                        w = wfc2[:, c, :] if L == 0 else par128[1][:, P128["fc2"] + C * c:P128["fc2"] + C * (c + 1)]
                        mm = pe.matmul(g[0:PT, p * step:p * step + width], hid[:, c, t], w, start=(c == 0), stop=(c == HCH - 1))
                    if L == 0:
                        mm = pe.matmul(g[0:PT, p * step + C + 1:(p + 1) * step], hid_ss[:, t], mean_w[:, 0:1],
                                       start=True, stop=True)
                mm.then_inc(s_f2[L], 1)

            def body(i):
                scores(i, 0, 0)
                scores(i, 0, 1)
                xT(i, "A1")
                qk(i, 1, "q", 0, s_q)
                qk(i, 1, "k", 1, s_k)
                probs_turn(i, 0, 0)
                v(i, 1, 0)
                v(i, 1, 1)
                attend(i, 0, 0)
                probs_turn(i, 0, 1)
                xT(i, "M1")
                fc1(i, 1, 0)
                attend(i, 0, 1)
                fc1(i, 1, 1)
                fc1(i, 1, 2)
                scores(i, 1, 0)
                spread_den(i, 0)
                fc2(i, 1)
                scores(i, 1, 1)
                project(i, 0)
                probs_turn(i, 1, 0)
                scores(i, 1, 2)
                attend(i, 1, 0)
                probs_turn(i, 1, 1)
                scores(i, 1, 3)
                attend(i, 1, 1)
                xT(i, "M0")
                fc1(i, 0, 0)
                probs_turn(i, 1, 2)
                fc1(i, 0, 1)
                scores(i, 1, 4)
                attend(i, 1, 2)
                fc1(i, 0, 2)
                probs_turn(i, 1, 3)
                scores(i, 1, 5)
                attend(i, 1, 3)
                xT(i, "A0")
                probs_turn(i, 1, 4)
                qk(i, 0, "q", 0, s_q)
                qk(i, 0, "k", 1, s_k)
                attend(i, 1, 4)
                probs_turn(i, 1, 5)
                attend(i, 1, 5)
                spread_den(i, 1)
                fc2(i, 0)
                v(i, 0, 0)
                v(i, 0, 1)
                project(i, 1)

            iterate(pe, body)

        @block.scalar
        def _(act):
            def turned(i, n):
                x = Strip(i, LAG[n])
                if not x.exists(ns):
                    return
                act.wait_ge(s_xt[n], x.count(1, 1))
                a = n[0] == "A"
                users = [(s_v[1], LAG["A1"], 2, 2), (s_v[0], LAG["A0"], 2, 2)] if a else \
                    [(s_f1[1], MLAG[1], HCH, HCH), (s_f1[0], MLAG[0], HCH, HCH)]
                if before := user_before(i, users, [0, 0], 0 if n[1] == "1" else 1):
                    act.wait_ge(*before)
                g = ps_g[G.index("xt" + n) % 3]
                if a:
                    dst, src = xnT_a[:, :, :, :], free(g[0:C, 0:1], (TOK, 8), (0, 2), (1, TOK))
                else:
                    dst, src = xnT_m[:, :], g[0:C, 0:ST]
                act.activation(dst, src, ACT.Copy).then_inc(s_xe[n], 1)

            def q_out(i, L):
                x = Strip(i, LAG[f"A{L}"])
                if x.exists(ns):
                    act.wait_ge(s_q[L], x.count(1, 1))
                    if x.back().exists(ns):
                        act.wait_ge(s_s[L], x.back().count(UNITS[L], UNITS[L]))
                    act.activation(qT[L][:, :], ps_g[G.index(f"q{L}") % 3][0:C, 0:ST], ACT.Identity, bias=bqkv[L][:, 0:1])\
                       .then_inc(s_qe[L], 1)

            def k_out(i, L):
                x = Strip(i, LAG[f"A{L}"])
                if x.exists(ns):
                    act.wait_ge(s_k[L], x.count(1, 1))
                    if before := user_before(i, [(s_km[1], LAG["A1"], 1, 1), (s_km[0], LAG["A0"], 1, 1)], [0, 0], 1 - L):
                        act.wait_ge(*before)
                    act.activation(kT[:, :], ps_g[G.index(f"k{L}") % 3][0:C, 0:ST], ACT.Identity, bias=bqkv[L][:, 1:2])\
                       .then_inc(s_ke[L], 1)

            def exps(i, L, u):
                x = Strip(i, ULAG[L])
                if x.exists(ns):
                    _, _, at = unit_place(L, u)
                    act.wait_ge(s_sh[L], x.count(UNITS[L], u + 1))
                    if before := user_before(i, by_unit(s_pt), two, at):
                        act.wait_ge(*before)
                    act.activation(probs[at % 2][:, :], shifted[at % 2][:, :], ACT.Exp).then_inc(s_ex[L], 1)

            def probsT_out(i, L, u):
                x = Strip(i, ULAG[L])
                if x.exists(ns):
                    _, _, at = unit_place(L, u)
                    act.wait_ge(s_pt[L], x.count(UNITS[L], u + 1))
                    if before := user_before(i, by_unit(s_pv), two, at):
                        act.wait_ge(*before)
                    act.activation(probsT[at % 2][:, :, :, :], free(ps_t[at % 2][0:PT, 0:1], (SP, 4), (64, 2), (1, TOK)),
                                   ACT.Copy).then_inc(s_pe[L], 1)

            def o_out(i, L):
                x = Strip(i, ULAG[L])
                if x.exists(ns):
                    act.wait_ge(s_pv[L], x.count(UNITS[L], UNITS[L]))
                    if before := user_before(i, [(s_on[0], ULAG[0], 1, 1), (s_on[1], ULAG[1], 1, 1)], [0, 0], L):
                        act.wait_ge(*before)
                    act.activation(o_raw[:, :], ps_o[0:OROWS, 0:ST], ACT.Copy).then_inc(s_oe[L], 1)

            def gelu(i, L, c):
                x = Strip(i, MLAG[L])
                if x.exists(ns):
                    act.wait_ge(s_f1[L], x.count(HCH, c + 1))
                    if c == 0:
                        if before := user_before(i, [(s_f2[1], MLAG[1], 1, 1), (s_f2[0], MLAG[0], 1, 1)], [0, 0], 1 - L):
                            act.wait_ge(*before)
                    act.activation(hid[:, c, :], ps_g[G.index(f"f1_{c}_{L}") % 3][:, 0:ST], ACT.Gelu, bias=bfc1[L][:, c:c + 1])\
                       .then_inc(s_ge[L], 1)

            def keep(i):
                x = Strip(i, 2)
                if x.exists(ns):
                    act.wait_ge(s_fin[0], x.count(1, 1))
                    if x.back().exists(ns):
                        act.wait_ge(s_xo[1], x.back().count(1, 1))
                    act.activation(x_keep[:, :, :], x_next[:, :, :], ACT.Copy).then_inc(s_keep, 1)

            def body(i):
                turned(i, "A1")
                exps(i, 0, 0)
                q_out(i, 1)
                k_out(i, 1)
                exps(i, 0, 1)
                probsT_out(i, 0, 0)
                keep(i)
                probsT_out(i, 0, 1)
                turned(i, "M1")
                gelu(i, 1, 0)
                gelu(i, 1, 1)
                o_out(i, 0)
                gelu(i, 1, 2)
                exps(i, 1, 0)
                exps(i, 1, 1)
                probsT_out(i, 1, 0)
                probsT_out(i, 1, 1)
                exps(i, 1, 2)
                turned(i, "M0")
                exps(i, 1, 3)
                gelu(i, 0, 0)
                probsT_out(i, 1, 2)
                gelu(i, 0, 1)
                gelu(i, 0, 2)
                probsT_out(i, 1, 3)
                exps(i, 1, 4)
                turned(i, "A0")
                probsT_out(i, 1, 4)
                exps(i, 1, 5)
                q_out(i, 0)
                k_out(i, 0)
                probsT_out(i, 1, 5)
                o_out(i, 1)

            act.wait_ge(s_w, 15)
            iterate(act, body)

        @block.vector
        def _(dve):
            dve.memset(ones[:, :], 1.0).then_inc(s_memset, 1)
            dve.memset(mean_w[:, :], 1.0 / HID).then_inc(s_memset, 1)
            dve.memset(minus_half[:, :], -0.5).then_inc(s_memset, 1)
            dve.memset(ps_o[:, :], 0.0).then_inc(s_memset, 1)
            dve.wait_ge(s_memset, 4)
            dve.wait_ge(s_const, NCONST)
            step = [0]

            def done(ins, wait=True):
                step[0] += 1
                ins.then_inc(s_w, 1)
                if wait:
                    dve.wait_ge(s_w, step[0])

            for L in (0, 1):
                p = par96[L]
                dve.wait_ge(s_wps, L + 1)
                done(dve.tensor_tensor(bqkv[L][:, :], ps_g[L][0:C, 0:3], p[:, P96["bqkv"]:P96["bqkv"] + 3], ALU.add))
                done(dve.tensor_scalar(bqkv[L][:, 0:1], bqkv[L][:, 0:1], float(HD[L]) ** -0.5, None, ALU.mult))
            g3 = free(par128[0][:, P128["g3"]:P128["g3"] + 1], (1, HCH), (0, C))
            w2 = par128[0][:, P128["fc2"]:P128["fc2"] + HCH * C]
            done(dve.tensor_tensor(wg3[:, :].rearrange("p (n c) -> p n c", n=HCH), w2.rearrange("p (n c) -> p n c", n=HCH),
                                   g3, ALU.mult))
            done(dve.tensor_copy(wfc2[:, :, C:C + 1], free(mean_w[:, 0:1], (1, HCH), (1, 1))))
            done(dve.tensor_copy(hid_sq[:, :, 0:PT], free(par128[0][:, P128["b3"]:P128["b3"] + 1], (1, HCH), (0, PT))))
            for L in (0, 1):
                p = par96[L]
                done(dve.tensor_scalar(wqkv[L][:, :], p[:, P96["qkv"]:P96["qkv"] + 3 * C], p[:, P96["g1"]:P96["g1"] + 1],
                                       None, ALU.mult))
            for L in (0, 1):
                dve.wait_ge(s_wps, 3 + L)
                done(dve.tensor_tensor(brow[L][0:1, :], ps_s[L][0:1, 0:C], rows[L][0:1, 0:C], ALU.add))
            for L in (0, 1):
                p = par96[L]
                dve.tensor_scalar(wfc1[L][:, :], p[:, P96["fc1"]:P96["fc1"] + HID], p[:, P96["g2"]:P96["g2"] + 1],
                                  None, ALU.mult)
                dve.tensor_tensor(bfc1[L][:, :], ps_g[L][:, 3:3 + HCH], par128[L][:, P128["bfc1"]:P128["bfc1"] + HCH], ALU.add)
                done(dve.tensor_scalar(wqkv[L][:, 0:C], wqkv[L][:, 0:C], float(HD[L]) ** -0.5, None, ALU.mult))
            dve.wait_ge(s_wps, 5)
            dve.tensor_tensor(wfc2[:, :, 0:C], wg3[:, :].rearrange("p (n c) -> p n c", n=HCH),
                              free(ps_g[2][:, 0:1], (0, HCH), (1, C)), ALU.subtract)
            dve.wait_ge(s_wps, 6)
            for L in (0, 1):
                dve.tensor_copy(bfc2[L][:, :], ps_t[L][0:PT, 0:C])
            done(dve.tensor_copy(t_high[:, :], t_in[:, :]))
            dve.tensor_copy(tleft[:, :], tleft_in[:, :])
            done(dve.scalar_tensor_tensor(out=table[:, :], in0=t_high[:, :].bitcast(f32), scalar=tlow[:, 0:1], in1=t_in[:, :],
                                          op0=ALU.mult, op1=ALU.add))

            def stats(i, n, off, src, ready, ready_per):
                x = Strip(i, off)
                if not x.exists(ns):
                    return
                dve.wait_ge(ready, x.count(ready_per, ready_per))
                if x.back().exists(ns):
                    dve.wait_ge(s_xn[n], x.back().count(1, 1))
                for p in range(PAIRS):
                    ins = dve.bn_stats(bn[n][:, p, :], src[:, p, :])
                ins.then_inc(s_bn[n], 1)
                dve.wait_ge(s_bn[n], x.count(2, 1))
                dve.memset(gate[:, :], 0.0)
                for p in range(PAIRS):
                    ins = dve.bn_aggr(mv[n][:, p, :], bn[n][:, p, :])
                ins.then_inc(s_bn[n], 1)
                dve.wait_ge(s_bn[n], x.count(2, 2))
                dve.tensor_scalar(var_eps[n][:, :], free(mv[n][:, 0, 1:2], (2, PAIRS)), EPS, None, ALU.add)\
                   .then_inc(s_var[n], 1)

            def v_out(i, L, half):
                x = Strip(i, LAG[f"A{L}"])
                if not x.exists(ns):
                    return
                dve.wait_ge(s_v[L], x.count(2, half + 1))
                if x.back().exists(ns):
                    dve.wait_ge(s_pv[L], x.back().count(UNITS[L], UNITS[L]))
                g = ps_g[G.index(("va", "vb")[half] + str(L)) % 3][0:PT, 0:1]
                base = vM[L][:, 4 * half, 0, 0:1]
                if L == 0:
                    n = 2 * HD[0]
                    src, dst = free(g, (n, 8), (1, n)), free(base, (VW[0], 8), (1, n))
                    mask = free(vmask[:, 0:1], (0, 8), (1, n))
                else:
                    n = 2 * HD[1]
                    src = free(g, (3 * n, 8), (n, 3), (1, n))
                    dst = free(base, (3 * VW[1], 8), (VW[1] + n, 3), (1, n))
                    mask = free(vmask[:, 2 * HD[0]:2 * HD[0] + 1], (0, 8), (0, 3), (1, n))
                dve.tensor_tensor(dst, src, mask, ALU.mult).then_inc(s_vm[L], 1)

            def norm(i, n, off, src):
                x = Strip(i, off)
                if not x.exists(ns):
                    return
                dve.wait_ge(s_rstd[n], x.count(1, 1))
                if x.back().exists(ns):
                    dve.wait_ge(s_xt[n], x.back().count(1, 1))
                for p in range(PAIRS):
                    ins = dve.tensor_scalar(xn[n][:, p, :], src[:, p, :], mv[n][:, p, 0:1], rstd[n][:, p:p + 1],
                                            ALU.subtract, ALU.mult)
                ins.then_inc(s_xn[n], 1)

            def variants(i, L):
                x = Strip(i, LAG[f"A{L}"])
                if not x.exists(ns):
                    return
                dve.wait_ge(s_ke[L], x.count(1, 1))
                if x.back().exists(ns):
                    dve.wait_ge(s_s[L], x.back().count(UNITS[L], UNITS[L]))
                for m in range(4):
                    ins = dve.tensor_scalar(kM[L][:, m, :], kT[:, :], kmask[:, 4 * L + m:4 * L + m + 1], None, ALU.mult)
                ins.then_inc(s_km[L], 1)

            def shift(i, L, u):
                x = Strip(i, ULAG[L])
                if not x.exists(ns):
                    return
                _, _, at = unit_place(L, u)
                dve.wait_ge(s_s[L], x.count(UNITS[L], u + 1))
                s = ps_s[at % 2][0:SP, 0:8 * TOK].rearrange("p (h k) -> p h k", k=TOK)
                nm = negmax[at % 2]
                dve.tensor_reduce(nm[:, :], s, AX.X, ALU.max, negate=True).then_inc(s_mx[L], 1)
                dve.wait_ge(s_mx[L], x.count(UNITS[L], u + 1))
                if before := user_before(i, by_unit(s_ex), two, at):
                    dve.wait_ge(*before)
                dve.tensor_tensor(shifted[at % 2][:, :].rearrange("p (h k) -> p h k", k=TOK), s,
                                  free(nm[:, 0:1], (1, 8), (0, TOK)), ALU.add).then_inc(s_sh[L], 1)

            def normalise(i, L):
                x = Strip(i, ULAG[L])
                if x.exists(ns):
                    dve.wait_ge(s_sp[L], x.count(1, 1))
                    dve.reciprocal(o_rden[:, :], ps_g[G.index(f"sp{L}") % 3][0:OROWS, 0:ST]).then_inc(s_rd[L], 1)
                    dve.wait_ge(s_rd[L], x.count(1, 1))
                    if before := user_before(i, [(s_pj[0], ULAG[0], 1, 1), (s_pj[1], ULAG[1], 1, 1)], [0, 0], L):
                        dve.wait_ge(*before)
                    dve.tensor_tensor(o_norm[:, :], o_raw[:, :], o_rden[:, :], ALU.mult).then_inc(s_on[L], 1)

            def residual(i, L):
                x = Strip(i, ULAG[L])
                if x.exists(ns):
                    dve.wait_ge(s_pj[L], x.count(1, 1))
                    if x.back().exists(ns):
                        dve.wait_ge(s_xb[L], x.back().count(1, 1))
                    if L == 1:
                        dve.wait_ge(s_keep, x.count(1, 1))
                    g = ps_g[G.index(f"pj{L}") % 3][0:PT, 0:PAIRS * C].rearrange("p (n c) -> p n c", c=C)
                    dst, src = ((x_mid0, x_in), (x_mid1, x_keep))[L]
                    dve.tensor_tensor(dst[:, :, :], src[:, :, :], g, ALU.add).then_inc(s_xo[L], 1)

            def finish1(i):
                x = Strip(i, MLAG[1])
                if x.exists(ns):
                    dve.wait_ge(s_f2[1], x.count(1, 1))
                    dve.wait_ge(s_xb[1], x.count(1, 1))
                    if x.back().exists(ns):
                        dve.wait_ge(s_store, x.back().count(16, 16))
                    g = ps_g[G.index("f2_1") % 3][0:PT, 0:PAIRS * C].rearrange("p (n c) -> p n c", c=C)
                    dve.tensor_tensor(y_out[:, :, :], x_biased[1][:, :, :], g, ALU.add).then_inc(s_fin[1], 1)

            def finish0(i):
                x = Strip(i, MLAG[0])
                if not x.exists(ns):
                    return
                dve.wait_ge(s_f2[0], x.count(1, 1))
                g = ps_g[G.index("f2_0") % 3]
                dve.tensor_copy(st3[:, :, :], free(g[0:PT, C:C + 1], (C + 2, PAIRS), (1, 2))).then_inc(s_v3, 1)
                dve.wait_ge(s_v3, x.count(4, 1))
                dve.scalar_tensor_tensor(out=var3[:, :], in0=st3[:, :, 0], scalar=-1.0, in1=st3[:, :, 0],
                                         op0=ALU.mult, op1=ALU.mult).then_inc(s_v3, 1)
                dve.wait_ge(s_v3, x.count(4, 2))
                dve.tensor_tensor(var3[:, :], var3[:, :], st3[:, :, 1], ALU.add).then_inc(s_v3, 1)
                dve.wait_ge(s_v3, x.count(4, 3))
                dve.tensor_scalar(var3[:, :], var3[:, :], 0.0, EPS, ALU.max, ALU.add).then_inc(s_v3, 1)
                dve.wait_ge(s_v3, x.count(4, 4))
                dve.wait_ge(s_rstd3, x.count(1, 1))
                dve.wait_ge(s_xb[0], x.count(1, 1))
                if x.back().exists(ns):
                    dve.wait_ge(s_keep, x.back().count(1, 1))
                for p in range(PAIRS):
                    ins = dve.scalar_tensor_tensor(out=x_next[:, p, :], in0=g[0:PT, p * (C + 2):p * (C + 2) + C],
                                                   scalar=rstd3[:, p:p + 1], in1=x_biased[0][:, p, :],
                                                   op0=ALU.mult, op1=ALU.add)
                ins.then_inc(s_fin[0], 1)

            def body(i):
                shift(i, 0, 0)
                stats(i, "M1", 3, x_mid1, s_xo[1], 1)
                shift(i, 0, 1)
                variants(i, 1)
                norm(i, "M1", 3, x_mid1)
                v_out(i, 1, 0)
                v_out(i, 1, 1)
                shift(i, 1, 0)
                normalise(i, 0)
                finish1(i)
                shift(i, 1, 1)
                residual(i, 0)
                stats(i, "M0", 1, x_mid0, s_xo[0], 1)
                shift(i, 1, 2)
                norm(i, "M0", 1, x_mid0)
                shift(i, 1, 3)
                stats(i, "A0", 0, x_in, s_load, 16)
                shift(i, 1, 4)
                norm(i, "A0", 0, x_in)
                shift(i, 1, 5)
                variants(i, 0)
                normalise(i, 1)
                finish0(i)
                stats(i, "A1", 1, x_next, s_fin[0], 1)
                v_out(i, 0, 0)
                v_out(i, 0, 1)
                norm(i, "A1", 1, x_next)
                residual(i, 1)

            iterate(dve, body)

        @block.gpsimd
        def _(pool):
            def inverse_root(i, n, off):
                x = Strip(i, off)
                if x.exists(ns):
                    pool.wait_ge(s_var[n], x.count(1, 1))
                    if x.back().exists(ns):
                        pool.wait_ge(s_xn[n], x.back().count(1, 1))
                    pool.tensor_tensor(rstd[n][:, :], var_eps[n][:, :], minus_half[:, :], ALU.pow).then_inc(s_rstd[n], 1)

            def add_bias(i, L, off, src):
                x = Strip(i, off)
                if x.exists(ns):
                    pool.wait_ge(s_xo[L], x.count(1, 1))
                    if x.back().exists(ns):
                        pool.wait_ge(s_fin[L], x.back().count(1, 1))
                    pool.tensor_tensor(x_biased[L][:, :, :], src[:, :, :], free(bfc2[L][:, 0:1], (0, PAIRS), (1, C)), ALU.add)\
                        .then_inc(s_xb[L], 1)

            def squares(i):
                x = Strip(i, MLAG[0])
                if not x.exists(ns):
                    return
                pool.wait_ge(s_ge[0], x.count(HCH, HCH))
                if x.back().exists(ns):
                    pool.wait_ge(s_f2[0], x.back().count(1, 1))
                pool.tensor_tensor(hid_sq[:, :, :], hid[:, :, :], hid[:, :, :], ALU.mult).then_inc(s_sq, 1)
                pool.wait_ge(s_sq, x.count(3, 1))
                pool.tensor_tensor(hid_ss[:, :], hid_sq[:, 0, :], hid_sq[:, 1, :], ALU.add).then_inc(s_sq, 1)
                pool.wait_ge(s_sq, x.count(3, 2))
                pool.tensor_tensor(hid_ss[:, :], hid_ss[:, :], hid_sq[:, 2, :], ALU.add).then_inc(s_sq, 1)

            def rstd_of_third(i):
                x = Strip(i, MLAG[0])
                if x.exists(ns):
                    pool.wait_ge(s_v3, x.count(4, 4))
                    if x.back().exists(ns):
                        pool.wait_ge(s_fin[0], x.back().count(1, 1))
                    pool.tensor_tensor(rstd3[:, :], var3[:, :], minus_half[:, :], ALU.pow).then_inc(s_rstd3, 1)

            def body(i):
                inverse_root(i, "M1", 3)
                add_bias(i, 1, 3, x_mid1)
                inverse_root(i, "M0", 1)
                add_bias(i, 0, 1, x_mid0)
                inverse_root(i, "A0", 0)
                squares(i)
                rstd_of_third(i)
                inverse_root(i, "A1", 1)

            pool.wait_ge(s_w, 15)
            iterate(pool, body)


def _strips(x):
    x = np.roll(x, (-SHIFT, -SHIFT), axis=(1, 2))
    b = x.shape[0]
    x = x.reshape(b, 8, WS, PAIRS, 2, WS, C)
    return np.ascontiguousarray(x.transpose(1, 0, 4, 2, 5, 3, 6)).reshape(8 * b, PT, PAIRS * C)


def _image(y, b):
    y = y.reshape(8, b, 2, WS, WS, PAIRS, C).transpose(1, 0, 3, 5, 2, 4, 6).reshape(b, 8 * WS, 8 * WS, C)
    return np.ascontiguousarray(np.roll(y, (SHIFT, SHIFT), axis=(1, 2)))


def _table(t):
    c = np.stack(np.meshgrid(np.arange(WS), np.arange(WS), indexing="ij")).reshape(2, -1)
    rel = c[:, :, None] - c[:, None, :] + WS - 1
    return t[rel[0] * (2 * WS - 1) + rel[1]].transpose(0, 2, 1).reshape(TOK, -1)


def host_arrays(inp):
    a = {"x": _strips(inp["x"])}
    tab = np.concatenate([_table(inp["L0_conv_rpb_table"]), _table(inp["L1_conv_rel_bias_table"])], 1)
    a["tab"] = np.concatenate([tab, tab], 0)
    names = [dict(g1="ln1_g", b1="ln1_b", g2="ln2_g", b2="ln2_b", w1="fc1_w", c1="fc1_b", w2="fc2_w", c2="fc2_b"),
             dict(g1="norm1_w", b1="norm1_b", g2="norm2_w", b2="norm2_b", w1="mlp_w1", c1="mlp_b1", w2="mlp_w2", c2="mlp_b2")]
    for L in (0, 1):
        get = lambda n: inp[f"L{L}_conv_{names[L].get(n, n)}"]
        col = lambda v: v[:, None]
        a[f"par96_{L}"] = np.concatenate(
            [col(get("g1")), col(get("b1")), get("qkv_b").reshape(3, C).T, col(get("g2")), col(get("b2")),
             get("qkv_w"), get("w1"), get("proj_w")], 1)
        chunks = lambda v: v.reshape(HCH, 128).T
        norm3 = [chunks(get("ln3_g")), chunks(get("ln3_b"))] if L == 0 else [np.zeros((128, 2 * HCH), np.float32)]
        a[f"par128_{L}"] = np.concatenate(
            norm3 + [chunks(get("c1")), get("w2").reshape(HCH, 128, C).transpose(1, 0, 2).reshape(128, -1)], 1)
        a[f"rows{L}"] = np.concatenate([get("proj_b"), get("c2")])[None]
        w = np.zeros((OROWS, C), np.float32)
        w[0:TCH], w[64:64 + TCH] = get("proj_w")[:TCH], get("proj_w")[TCH:]
        a[f"wproj{L}"] = w
    a.update(shape_constants())
    return {n: np.ascontiguousarray(v) for n, v in a.items()}


def kernel(**inputs):
    import concourse.bacc as _bacc
    from concourse import mybir as _mybir
    from concourse.bass_utils import run_bass_kernel_spmd as _run

    arrays = host_arrays({n: np.asarray(v) for n, v in inputs.items()})
    nc = _bacc.Bacc("TRN2", target_bir_lowering=False, num_devices=1)
    d = {n: nc.dram_tensor(f"in_{n}", a.shape, _mybir.dt.from_np(a.dtype), kind="ExternalInput").ap()
         for n, a in arrays.items()}
    out = nc.dram_tensor("out_y", arrays["x"].shape, _mybir.dt.float32, kind="ExternalOutput").ap()
    swin_program(nc, d, out)
    r = _run(nc, [{f"in_{n}": a for n, a in arrays.items()}], core_ids=[0])
    return _image(np.asarray(r.results[0]["out_y"]), inputs["x"].shape[0])
```

```python
import concourse.bass as bass
from concourse import mybir
from contextlib import ExitStack
import numpy as np

LAST = 3
NSTRIP, ROWS_IN_IMAGE = 256, 8
WS, SHIFT = 7, 3
TOK = WS * WS
HALF = (0, 64)
SP = 64 + TOK
PAIRS = 4
PT = 2 * TOK
ST = PAIRS * PT
C, HID, HCH = 96, 384, 3
NH = (4, 12)
HD = (C // NH[0], C // NH[1])
UNITS = (NH[0] // 4 * 2, NH[1] // 4 * 2)
NHP = (NH[0] // 2, NH[1] // 2)
TCH = C // 2
VW = tuple(TCH + n // 2 for n in NH)
OROWS = 64 + max(VW)
EPS = 1e-5
NREG = 6
BK = 2 * TOK + NREG


def _regions():
    r = (np.arange(WS) >= WS - SHIFT).astype(int)
    return np.repeat(r, WS), np.tile(r, WS)


def shape_constants():
    rr, rc = _regions()
    k = {}
    k["ident"] = np.eye(128, dtype=np.float32)
    c = np.arange(C)
    k["kmask"] = np.stack([(c // HD[0])[:, None] == np.arange(4), (c % 32 // HD[1])[:, None] == np.arange(4)], 1)\
        .reshape(C, 8).astype(np.float32)
    rep = (np.arange(PT) // TOK)[:, None]
    k["vmask"] = np.concatenate([(np.arange(2 * HD[L]) // HD[L])[None] == rep for L in (0, 1)], 1).astype(np.float32)
    for L in (0, 1):
        v = np.zeros((PT, 8, NHP[L], VW[L]), np.float32)
        for hp in range(NHP[L]):
            local = hp % (NHP[L] // 2)
            for r in (0, 1):
                v[r * TOK:(r + 1) * TOK, :, hp, TCH + 2 * local + r] = 1
        k[f"vinit{L}"] = v.reshape(PT, -1)
        e = np.zeros((OROWS, OROWS), np.float32)
        for r in range(OROWS):
            t, cc = divmod(r, 64)
            if cc < TCH:
                e[64 * t + TCH + cc // HD[L], r] = 1
            elif cc < VW[L]:
                e[r, r] = 1
            else:
                e[TCH, r] = 1
        k[f"spread{L}"] = e
    left = np.zeros((BK, 2, SP), np.float32)
    for part in (0, 1):
        for h in HALF:
            left[part * TOK + np.arange(TOK), :, h + np.arange(TOK)] = 1
    for q in range(TOK):
        left[2 * TOK + rr[q], :, HALF[0] + q] = 1
        left[2 * TOK + rr[q], 0, HALF[1] + q] = 1
        left[2 * TOK + 2 + 2 * rr[q] + rc[q], 1, HALF[1] + q] = 1
    k["tleft"] = left.reshape(BK, -1)
    right = np.zeros((NREG, 2, sum(NH), TOK), np.float32)
    for g in (0, 1):
        right[g, 1] = -100.0 * (rr != g)
        for h in (0, 1):
            right[2 + 2 * g + h, 0] = -100.0 * (rc != h)
            right[2 + 2 * g + h, 1] = -100.0 * ((rr != g) | (rc != h))
    k["tmask"] = right.reshape(NREG, -1)
    k["tlow"] = -(np.arange(BK) // TOK == 1).astype(np.float32)[:, None]
    return k


class Strip:

    def __init__(self, i, off):
        self.i, self.off = i, off
        self.known = isinstance(i, int)

    def back(self, n=1):
        return Strip(self.i, self.off + n)

    def exists(self, n):
        return not self.known or 0 <= self.i - self.off < n

    def count(self, per, c):
        return (self.i - self.off) * per + c if self.known else self.i * per + (c - self.off * per)


def swin_program(nc, d, out, ns=NSTRIP, last_row_from=NSTRIP - NSTRIP // ROWS_IN_IMAGE):
    f32, f32r = mybir.dt.float32, mybir.dt.float32r
    ALU, ACT, AX = mybir.AluOpType, mybir.ActivationFunctionType, mybir.AxisListType
    assert (last_row_from + 256) >= 0
    ctx = ExitStack()
    with ctx:
        def sb(name, shape, dt=f32):
            return ctx.enter_context(nc.sbuf_tensor(name, shape, dt))

        def bank(name, shape=(128, 512)):
            return ctx.enter_context(nc.psum_tensor(name, list(shape), f32))

        def sem(name):
            return ctx.enter_context(nc.semaphore(name))

        def free(ap, *dims):
            return bass.AP(ap.tensor, ap.offset, [list(ap.ap[0])] + [list(x) for x in dims])

        ident = sb("ident", [128, 128])
        kmask = sb("kmask", [C, 8])
        vmask = sb("vmask", [PT, 2 * HD[0] + 2 * HD[1]])
        spread = [sb(f"spread{L}", [OROWS, OROWS]) for L in (0, 1)]
        tleft_in = sb("tleft_in", [BK, 2 * SP])
        tlow = sb("tlow", [BK, 1])
        NT = TOK * sum(NH)
        t_in = sb("t_in", [BK, 2 * NT])
        t_high = sb("t_high", [BK, 2 * NT], f32r)
        tleft = sb("tleft", [BK, 2 * SP], f32r)
        table = sb("table", [BK, 2 * NT], f32r)
        NP96 = 7 + 3 * C + HID + C
        par96 = [sb(f"par96_{L}", [C, NP96]) for L in (0, 1)]
        NP128 = 9 + HCH * C
        par128 = [sb(f"par128_{L}", [128, NP128]) for L in (0, 1)]
        rows = [sb(f"rows{L}", [1, 2 * C]) for L in (0, 1)]
        wqkv = [sb(f"wqkv{L}", [C, 3 * C]) for L in (0, 1)]
        bqkv = [sb(f"bqkv{L}", [C, 3]) for L in (0, 1)]
        wproj = [sb(f"wproj{L}", [OROWS, C]) for L in (0, 1)]
        brow = [sb(f"brow{L}", [1, C]) for L in (0, 1)]
        wfc1 = [sb(f"wfc1_{L}", [C, HID]) for L in (0, 1)]
        bfc1 = [sb(f"bfc1_{L}", [128, HCH]) for L in (0, 1)]
        wg3 = sb("wg3", [128, HCH * C])
        wfc2 = sb("wfc2", [128, HCH, C + 1])
        ones = sb("ones", [128, 128])
        mean_w = sb("mean_w", [128, 128])
        bfc2 = [sb(f"bfc2_{L}", [PT, C]) for L in (0, 1)]

        x_in = sb("x_in", [PT, PAIRS, C])
        x_mid0 = sb("x_mid0", [PT, PAIRS, C])
        x_next = sb("x_next", [PT, PAIRS, C])
        x_keep = sb("x_keep", [PT, PAIRS, C])
        x_mid1 = sb("x_mid1", [PT, PAIRS, C])
        x_biased = [sb(f"x_biased{L}", [PT, PAIRS, C]) for L in (0, 1)]
        y_out = sb("y_out", [PT, PAIRS, C])
        LN = ("A0", "M0", "A1", "M1")
        bn = {n: sb("bn" + n, [PT, PAIRS, 6]) for n in LN}
        mv = {n: sb("mv" + n, [PT, PAIRS, 2]) for n in LN}
        var_eps = {n: sb("var_eps" + n, [PT, PAIRS]) for n in LN}
        gate = sb("gate", [1, 1])
        minus_half = sb("minus_half", [PT, PAIRS])
        rstd = {n: sb("rstd" + n, [PT, PAIRS]) for n in LN}
        xn = {n: sb("xn" + n, [PT, PAIRS, C]) for n in LN}
        xnT_a = [sb(f"xnT_a{L}", [C, 8, 2, TOK]) for L in (0, 1)]
        xnT_m = [sb(f"xnT_m{L}", [C, ST]) for L in (0, 1)]
        qT = [sb(f"qT{L}", [C, ST]) for L in (0, 1)]
        kT = [sb(f"kT{L}", [C, ST]) for L in (0, 1)]
        kM = [sb(f"kM{L}", [C, 4, ST]) for L in (0, 1)]
        vM = [sb(f"vM{L}", [PT, 8, NHP[L], VW[L]]) for L in (0, 1)]
        negmax = [sb(f"negmax{n}", [SP, 8]) for n in (0, 1)]
        shifted = [sb(f"shifted{n}", [SP, 2 * 4 * TOK]) for n in (0, 1)]
        probs = [sb(f"probs{n}", [SP, 2 * 4 * TOK]) for n in (0, 1)]
        probsT = [sb(f"probsT{n}", [PT, 4, 2, TOK]) for n in (0, 1)]
        o_raw = [sb(f"o_raw{L}", [OROWS, ST]) for L in (0, 1)]
        o_rden = sb("o_rden", [OROWS, ST])
        o_norm = [sb(f"o_norm{L}", [OROWS, ST]) for L in (0, 1)]
        hid = [sb(f"hid{L}", [128, HCH, ST]) for L in (0, 1)]
        hid_sq = sb("hid_sq", [128, HCH, ST])
        hid_ss = sb("hid_ss", [128, ST])
        st3 = sb("st3", [PT, PAIRS, 2])
        var3 = sb("var3", [PT, PAIRS])
        rstd3 = sb("rstd3", [PT, PAIRS])

        ps_s = [bank(f"ps_s{n}") for n in range(2)]
        ps_t = [bank(f"ps_t{n}") for n in range(2)]
        ps_o = bank("ps_o")
        ps_g = [bank(f"ps_g{n}") for n in range(3)]

        s_const = sem("s_const")
        s_memset = sem("s_memset")
        s_w = sem("s_w")
        s_wps = sem("s_wps")
        s_brow = sem("s_brow")
        s_load = sem("s_load")
        s_store = sem("s_store")
        s_bn = {n: sem("s_bn" + n) for n in LN}
        s_var = {n: sem("s_var" + n) for n in LN}
        s_rstd = {n: sem("s_rstd" + n) for n in LN}
        s_xn = {n: sem("s_xn" + n) for n in LN}
        s_xt = {n: sem("s_xt" + n) for n in LN}
        s_xe = {n: sem("s_xe" + n) for n in LN}
        pairsem = lambda name: [sem(f"{name}{L}") for L in (0, 1)]
        s_q, s_qe = pairsem("s_q"), pairsem("s_qe")
        s_k, s_ke = pairsem("s_k"), pairsem("s_ke")
        s_km = pairsem("s_km")
        s_v, s_vm = pairsem("s_v"), pairsem("s_vm")
        s_s = pairsem("s_s")
        s_mx = pairsem("s_mx")
        s_sh = pairsem("s_sh")
        s_ex = pairsem("s_ex")
        s_pt, s_pe = pairsem("s_pt"), pairsem("s_pe")
        s_pv = pairsem("s_pv")
        s_oe = pairsem("s_oe")
        s_sp = pairsem("s_sp")
        s_rd = pairsem("s_rd")
        s_on = pairsem("s_on")
        s_pj = pairsem("s_pj")
        s_xo = pairsem("s_xo")
        s_xb = pairsem("s_xb")
        s_f1, s_ge = pairsem("s_f1"), pairsem("s_ge")
        s_sq = sem("s_sq")
        s_f2 = pairsem("s_f2")
        s_v3 = sem("s_v3")
        s_rstd3 = sem("s_rstd3")
        s_fin = pairsem("s_fin")
        s_keep = sem("s_keep")

        G = [("vb0", 1), ("sp1", 3), ("xtA1", 2), ("q1", 2), ("pj1", 3), ("k1", 2), ("va1", 2), ("sp0", 1), ("xtM1", 3),
             ("f1_0_1", 3), ("pj0", 1), ("f1_1_1", 3), ("f1_2_1", 3), ("f2_1", 3), ("xtM0", 1), ("vb1", 2), ("f1_0_0", 1),
             ("f1_1_0", 1), ("f1_2_0", 1), ("xtA0", 0), ("q0", 0), ("k0", 0), ("va0", 0), ("f2_0", 1)]
        O = [(0, 1), (1, 2)]
        SCORES = [((0, 0), 1), ((0, 1), 1), ((1, 0), 2), ((1, 1), 2), ((1, 2), 2), ((1, 3), 2), ((1, 4), 2), ((1, 5), 2)]
        SHIFTS = [((1, 5), 3), ((0, 0), 1), ((0, 1), 1), ((1, 0), 2), ((1, 1), 2), ((1, 2), 2), ((1, 3), 2), ((1, 4), 2)]
        EXPS = [((1, 5), 3), ((0, 0), 1), ((0, 1), 1), ((1, 0), 2), ((1, 1), 2), ((1, 2), 2), ((1, 3), 2), ((1, 4), 2)]
        TURNS = [((1, 4), 3), ((1, 5), 3), ((0, 0), 1), ((0, 1), 1), ((1, 0), 2), ((1, 1), 2), ((1, 2), 2), ((1, 3), 2)]
        COPIES = [((1, 2), 3), ((1, 3), 3), ((1, 4), 3), ((1, 5), 3), ((0, 0), 1), ((0, 1), 1), ((1, 0), 2), ((1, 1), 2)]
        UNIT_ORDER = [use for use, _ in SCORES]
        place = lambda use: UNIT_ORDER.index(use) % 2

        over_g = {}
        for n in LN:
            over_g["xt" + n] = (s_xe[n], 1, 1)
        for L in (0, 1):
            over_g[f"q{L}"] = (s_qe[L], 1, 1)
            over_g[f"k{L}"] = (s_ke[L], 1, 1)
            over_g[f"va{L}"] = (s_vm[L], 2, 1)
            over_g[f"vb{L}"] = (s_vm[L], 2, 2)
            over_g[f"sp{L}"] = (s_rd[L], 1, 1)
            over_g[f"pj{L}"] = (s_xo[L], 1, 1)
            over_g[f"f2_{L}"] = (s_fin[L], 1, 1)
            for c in range(HCH):
                over_g[f"f1_{c}_{L}"] = (s_ge[L], HCH, c + 1)
        bank_of = {use: n % 3 for n, (use, _) in enumerate(G)}
        unit_over = lambda s: {(L, u): (s[L], UNITS[L], u + 1) for L, u in UNIT_ORDER}

        def before(x, ring, over, slot, use):
            at = [n for n, _ in ring].index(use)
            assert ring[at][1] == x.off
            wraps = 0
            for _ in range(4 * len(ring)):
                at -= 1
                if at < 0:
                    at, wraps = at + len(ring), wraps + 1
                other, lag = ring[at]
                y = Strip(x.i, lag + wraps)
                if slot(other) == slot(use) and y.exists(ns):
                    semaphore, per, c = over[other]
                    return semaphore, y.count(per, c)
            return None

        def g_before(x, use):
            return before(x, G, over_g, lambda n: bank_of[n], use)

        def unit_place(L, u):
            return u // (UNITS[L] // 2), u % (UNITS[L] // 2), place((L, u))

        NCONST = 0
        loads = [(ident[:, :], d["ident"]), (kmask[:, :], d["kmask"]), (vmask[:, :], d["vmask"]),
                 (tleft_in[:, :], d["tleft"]), (tlow[:, :], d["tlow"]),
                 (t_in[2 * TOK:BK, :], d["tmask"])]
        for v in (0, 1):
            loads.append((t_in[0:2 * TOK, v * NT:(v + 1) * NT], d["tab"]))
        for L in (0, 1):
            loads += [(spread[L][:, :], d[f"spread{L}"]), (par96[L][:, :], d[f"par96_{L}"]),
                      (par128[L][:, :], d[f"par128_{L}"]), (rows[L][:, :], d[f"rows{L}"]),
                      (wproj[L][:, :], d[f"wproj{L}"]),
                      (vM[L][:, :, :, :].rearrange("p w h c -> p (w h c)"), d[f"vinit{L}"])]
        NCONST = 16 * len(loads)
        P96 = {"g1": 0, "b1": 1, "bqkv": 2, "g2": 5, "b2": 6, "qkv": 7, "fc1": 7 + 3 * C, "proj": 7 + 3 * C + HID}
        P128 = {"g3": 0, "b3": 3, "bfc1": 6, "fc2": 9}

        def iterate(eng, body):
            total, first = ns + LAST, LAST + 2
            for i in range(min(first, total)):
                body(i)
            if ns > first:
                with eng.Fori(first, ns) as i:
                    body(i)
            for i in range(max(first, ns), total):
                body(i)

        block = ctx.enter_context(nc.Block())

        @block.sync
        def _(sp):
            for dst, src in loads:
                sp.dma_start(dst, src).then_inc(s_const, 16)
            for L in (0, 1):
                sp.wait_ge(s_w, 10 + L)
                sp.dma_start(wproj[L][TCH:TCH + 1, :], brow[L][0:1, :]).then_inc(s_brow, 16)

            def body(i):
                a0 = Strip(i, 0)
                if a0.exists(ns):
                    if a0.back().exists(ns):
                        sp.wait_ge(s_xo[0], a0.back().count(1, 1))
                    n = i if isinstance(i, int) else bass.ds(i, 1)
                    src = d["x"][n, :, :] if isinstance(i, int) else d["x"][n, :, :].rearrange("a p c -> (a p) c")
                    sp.dma_start(x_in[:, :, :].rearrange("p a c -> p (a c)"), src).then_inc(s_load, 16)
                m1 = Strip(i, 3)
                if m1.exists(ns):
                    sp.wait_ge(s_fin[1], m1.count(1, 1))
                    if isinstance(i, int):
                        dst = out[i - 3, :, :]
                    else:
                        dst = out[bass.ds(i - 3, 1), :, :].rearrange("a p c -> (a p) c")
                    sp.dma_start(dst, y_out[:, :, :].rearrange("p a c -> p (a c)")).then_inc(s_store, 16)

            iterate(sp, body)
            sp.wait_ge(s_store, 16 * ns)

        @block.tensor
        def _(pe):
            pe.wait_ge(s_const, NCONST)
            pe.wait_ge(s_memset, 4)
            for L in (0, 1):
                p = par96[L]
                for n in range(3):
                    pe.matmul(ps_g[L][0:C, n:n + 1], p[:, P96["qkv"] + C * n:P96["qkv"] + C * (n + 1)],
                              p[:, P96["b1"]:P96["b1"] + 1], start=True, stop=True)
                for n in range(HCH):
                    mm = pe.matmul(ps_g[L][:, 3 + n:4 + n], p[:, P96["fc1"] + 128 * n:P96["fc1"] + 128 * (n + 1)],
                                   p[:, P96["b2"]:P96["b2"] + 1], start=True, stop=True)
                mm.then_inc(s_wps, 1)
            for L in (0, 1):
                pe.wait_ge(s_w, 2 + 2 * L)
                pe.matmul(ps_s[L][0:1, 0:C], bqkv[L][:, 2:3], par96[L][:, P96["proj"]:P96["proj"] + C],
                          start=True, stop=True).then_inc(s_wps, 1)
            pe.wait_ge(s_w, 6)
            for c in range(HCH):
                mm = pe.matmul(ps_g[2][:, 0:C], mean_w[:, :], wg3[:, C * c:C * (c + 1)], start=(c == 0), stop=(c == HCH - 1))
            mm.then_inc(s_wps, 1)
            pe.wait_ge(s_w, 7)
            for c in range(HCH):
                pe.matmul(ps_t[0][0:PT, 0:C], hid_sq[:, c, 0:PT], par128[0][:, P128["fc2"] + C * c:P128["fc2"] + C * (c + 1)],
                          start=(c == 0), stop=False)
            pe.matmul(ps_t[0][0:PT, 0:C], ones[0:1, 0:PT], rows[0][0:1, C:2 * C], start=False, stop=True)
            pe.matmul(ps_t[1][0:PT, 0:C], ones[0:1, 0:PT], rows[1][0:1, C:2 * C], start=True, stop=True).then_inc(s_wps, 1)
            pe.wait_ge(s_w, 15)
            pe.wait_ge(s_brow, 32)

            def xT(x, n):
                if x.exists(ns):
                    pe.wait_ge(s_xn[n], x.count(1, 1))
                    use = "xt" + n
                    if free_from := g_before(x, use):
                        pe.wait_ge(*free_from)
                    g = ps_g[bank_of[use]]
                    for p in range(PAIRS):
                        mm = pe.transpose(g[0:C, p * PT:(p + 1) * PT], xn[n][:, p, :], ident[0:PT, 0:PT])
                    mm.then_inc(s_xt[n], 1)

            def qk(x, L, name, part, signal):
                if x.exists(ns):
                    pe.wait_ge(s_xe[f"A{L}"], x.count(1, 1))
                    use = f"{name}{L}"
                    if free_from := g_before(x, use):
                        pe.wait_ge(*free_from)
                    g = ps_g[bank_of[use]]
                    pe.matmul(g[0:C, 0:ST], wqkv[L][:, part * C:(part + 1) * C], xnT_a[L][:, :, 0, :], start=True, stop=True)\
                      .then_inc(signal[L], 1)

            def v(x, L, half):
                if x.exists(ns):
                    pe.wait_ge(s_xe[f"A{L}"], x.count(1, 1))
                    use = ("va", "vb")[half] + str(L)
                    if free_from := g_before(x, use):
                        pe.wait_ge(*free_from)
                    g = ps_g[bank_of[use]]
                    for n in range(4):
                        w = 4 * half + n
                        twice = xnT_a[L][:, w, :, :].rearrange("p r t -> p (r t)")
                        mm = pe.matmul(g[0:PT, n * C:(n + 1) * C], twice, wqkv[L][:, 2 * C:3 * C], start=True, stop=True)
                    mm.then_inc(s_v[L], 1)

            def scores(x, L, u):
                if not x.exists(ns):
                    return
                two_pairs, group, at = unit_place(L, u)
                if free_from := before(x, SCORES, unit_over(s_sh), place, (L, u)):
                    pe.wait_ge(*free_from)
                s = ps_s[at]
                pe.wait_ge(s_qe[L], x.count(1, 1))
                pe.wait_ge(s_km[L], x.count(1, 1))
                col = TOK * (4 * group + (NH[0] if L else 0))
                if x.known:
                    start = (1 if x.i - x.off >= last_row_from else 0) * NT + col
                    tab = table[:, start:start + 4 * TOK]
                else:
                    which = (x.i + (256 - last_row_from - x.off)) // 256
                    tab = table[:, bass.ds(which * NT + col, 4 * TOK)]
                for p in (0, 1):
                    left = 1 if 2 * two_pairs + p == PAIRS - 1 else 0
                    pe.matmul(s[0:SP, 4 * TOK * p:4 * TOK * (p + 1)], tleft[:, left * SP:(left + 1) * SP], tab,
                              start=(p == 0), stop=False, skip_group_check=True)
                r = slice(0, C) if L == 0 else slice(32 * group, 32 * group + 32)
                for p in (0, 1):
                    for h in (0, 1):
                        t = (2 * two_pairs + p) * PT + h * TOK
                        mm = pe.matmul(s[HALF[h]:HALF[h] + TOK, 4 * TOK * p:4 * TOK * (p + 1)], qT[L][r, t:t + TOK],
                                       kM[L][r, :, t:t + TOK], start=False, stop=True, skip_group_check=True)
                mm.then_inc(s_s[L], 1)

            def probs_turn(x, L, u):
                if not x.exists(ns):
                    return
                _, _, at = unit_place(L, u)
                pe.wait_ge(s_ex[L], x.count(UNITS[L], u + 1))
                if free_from := before(x, TURNS, unit_over(s_pe), place, (L, u)):
                    pe.wait_ge(*free_from)
                for n in range(4):
                    mm = pe.transpose(ps_t[at][0:PT, n * SP:(n + 1) * SP], probs[at][:, n * PT:(n + 1) * PT],
                                      ident[0:SP, 0:SP])
                mm.then_inc(s_pt[L], 1)

            def attend(x, L, u):
                if not x.exists(ns):
                    return
                two_pairs, group, at = unit_place(L, u)
                pe.wait_ge(s_pe[L], x.count(UNITS[L], u + 1))
                pe.wait_ge(s_vm[L], x.count(2, 2))
                if u == 0:
                    if free_from := before(x, O, {0: (s_oe[0], 1, 1), 1: (s_oe[1], 1, 1)}, lambda n: 0, L):
                        pe.wait_ge(*free_from)
                begun = set()
                for p in (0, 1):
                    for h in (0, 1):
                        w = 2 * (2 * two_pairs + p) + h
                        for n in (0, 1):
                            hp = 2 * group + n
                            tile = hp // (NHP[L] // 2)
                            first = u == {(0, 0): 0, (0, 1): 0, (1, 0): 0, (1, 1): 1}[L, tile] and tile not in begun
                            begun.add(tile)
                            mm = pe.matmul(ps_o[64 * tile:64 * tile + VW[L], w * TOK:(w + 1) * TOK], vM[L][:, w, hp, :],
                                           probsT[at][:, 2 * p + n, h, :], start=first, stop=True, skip_group_check=True)
                mm.then_inc(s_pv[L], 1)

            def spread_den(x, L):
                if x.exists(ns):
                    pe.wait_ge(s_oe[L], x.count(1, 1))
                    use = f"sp{L}"
                    if free_from := g_before(x, use):
                        pe.wait_ge(*free_from)
                    g = ps_g[bank_of[use]]
                    pe.matmul(g[0:OROWS, 0:ST], spread[L][:, :], o_raw[L][:, :], start=True, stop=True).then_inc(s_sp[L], 1)

            def project(x, L):
                if x.exists(ns):
                    pe.wait_ge(s_on[L], x.count(1, 1))
                    use = f"pj{L}"
                    if free_from := g_before(x, use):
                        pe.wait_ge(*free_from)
                    g = ps_g[bank_of[use]]
                    for p in range(PAIRS):
                        mm = pe.matmul(g[0:PT, p * C:(p + 1) * C], o_norm[L][:, p * PT:(p + 1) * PT], wproj[L][:, :],
                                       start=True, stop=True)
                    mm.then_inc(s_pj[L], 1)

            def fc1(x, L, c):
                if x.exists(ns):
                    pe.wait_ge(s_xe[f"M{L}"], x.count(1, 1))
                    use = f"f1_{c}_{L}"
                    if free_from := g_before(x, use):
                        pe.wait_ge(*free_from)
                    g = ps_g[bank_of[use]]
                    pe.matmul(g[:, 0:ST], wfc1[L][:, 128 * c:128 * (c + 1)], xnT_m[L][:, :], start=True, stop=True)\
                      .then_inc(s_f1[L], 1)

            def fc2(x, L):
                if not x.exists(ns):
                    return
                pe.wait_ge(s_ge[L], x.count(HCH, HCH))
                if L == 0:
                    pe.wait_ge(s_sq, x.count(3, 3))
                use = f"f2_{L}"
                if free_from := g_before(x, use):
                    pe.wait_ge(*free_from)
                g = ps_g[bank_of[use]]
                step, width = (C + 2, C + 1) if L == 0 else (C, C)
                for p in range(PAIRS):
                    t = slice(p * PT, (p + 1) * PT)
                    for c in range(HCH):
                        w = wfc2[:, c, :] if L == 0 else par128[1][:, P128["fc2"] + C * c:P128["fc2"] + C * (c + 1)]
                        mm = pe.matmul(g[0:PT, p * step:p * step + width], hid[L][:, c, t], w, start=(c == 0), stop=(c == HCH - 1))
                    if L == 0:
                        mm = pe.matmul(g[0:PT, p * step + C + 1:(p + 1) * step], hid_ss[:, t], mean_w[:, 0:1],
                                       start=True, stop=True)
                mm.then_inc(s_f2[L], 1)

            def body(i):
                s0, s1, s2, s3 = Strip(i, 0), Strip(i, 1), Strip(i, 2), Strip(i, 3)
                attend(s3, 1, 1)
                attend(s3, 1, 2)
                probs_turn(s3, 1, 4)
                probs_turn(s3, 1, 5)
                attend(s3, 1, 3)
                scores(s1, 0, 0)
                attend(s3, 1, 4)
                attend(s3, 1, 5)
                v(s1, 0, 1)
                spread_den(s3, 1)
                xT(s2, "A1")
                qk(s2, 1, "q", 0, s_q)
                scores(s1, 0, 1)
                probs_turn(s1, 0, 0)
                project(s3, 1)
                qk(s2, 1, "k", 1, s_k)
                attend(s1, 0, 0)
                probs_turn(s1, 0, 1)
                v(s2, 1, 0)
                attend(s1, 0, 1)
                spread_den(s1, 0)
                xT(s3, "M1")
                scores(s2, 1, 0)
                fc1(s3, 1, 0)
                scores(s2, 1, 1)
                project(s1, 0)
                fc1(s3, 1, 1)
                fc1(s3, 1, 2)
                scores(s2, 1, 2)
                fc2(s3, 1)
                xT(s1, "M0")
                v(s2, 1, 1)
                fc1(s1, 0, 0)
                fc1(s1, 0, 1)
                probs_turn(s2, 1, 0)
                fc1(s1, 0, 2)
                scores(s2, 1, 3)
                xT(s0, "A0")
                probs_turn(s2, 1, 1)
                scores(s2, 1, 4)
                attend(s2, 1, 0)
                scores(s2, 1, 5)
                qk(s0, 0, "q", 0, s_q)
                qk(s0, 0, "k", 1, s_k)
                v(s0, 0, 0)
                probs_turn(s2, 1, 2)
                fc2(s1, 0)
                probs_turn(s2, 1, 3)

            iterate(pe, body)

        @block.scalar
        def _(act):
            def turned(x, n):
                if not x.exists(ns):
                    return
                act.wait_ge(s_xt[n], x.count(1, 1))
                a = n[0] == "A"
                L = int(n[1])
                if x.back().exists(ns):
                    if a:
                        act.wait_ge(s_v[L], x.back().count(2, 2))
                    else:
                        act.wait_ge(s_f1[L], x.back().count(HCH, HCH))
                g = ps_g[bank_of["xt" + n]]
                if a:
                    dst, src = xnT_a[L][:, :, :, :], free(g[0:C, 0:1], (TOK, 8), (0, 2), (1, TOK))
                else:
                    dst, src = xnT_m[L][:, :], g[0:C, 0:ST]
                act.activation(dst, src, ACT.Copy).then_inc(s_xe[n], 1)

            def q_out(x, L):
                if x.exists(ns):
                    act.wait_ge(s_q[L], x.count(1, 1))
                    if x.back().exists(ns):
                        act.wait_ge(s_s[L], x.back().count(UNITS[L], UNITS[L]))
                    act.activation(qT[L][:, :], ps_g[bank_of[f"q{L}"]][0:C, 0:ST], ACT.Identity, bias=bqkv[L][:, 0:1])\
                       .then_inc(s_qe[L], 1)

            def k_out(x, L):
                if x.exists(ns):
                    act.wait_ge(s_k[L], x.count(1, 1))
                    if x.back().exists(ns):
                        act.wait_ge(s_km[L], x.back().count(1, 1))
                    act.activation(kT[L][:, :], ps_g[bank_of[f"k{L}"]][0:C, 0:ST], ACT.Identity, bias=bqkv[L][:, 1:2])\
                       .then_inc(s_ke[L], 1)

            def exps(x, L, u):
                if x.exists(ns):
                    _, _, at = unit_place(L, u)
                    act.wait_ge(s_sh[L], x.count(UNITS[L], u + 1))
                    if free_from := before(x, EXPS, unit_over(s_pt), place, (L, u)):
                        act.wait_ge(*free_from)
                    act.activation(probs[at][:, :], shifted[at][:, :], ACT.Exp).then_inc(s_ex[L], 1)

            def probsT_out(x, L, u):
                if x.exists(ns):
                    _, _, at = unit_place(L, u)
                    act.wait_ge(s_pt[L], x.count(UNITS[L], u + 1))
                    if free_from := before(x, COPIES, unit_over(s_pv), place, (L, u)):
                        act.wait_ge(*free_from)
                    act.activation(probsT[at][:, :, :, :], free(ps_t[at][0:PT, 0:1], (SP, 4), (64, 2), (1, TOK)),
                                   ACT.Copy).then_inc(s_pe[L], 1)

            def o_out(x, L):
                if x.exists(ns):
                    act.wait_ge(s_pv[L], x.count(UNITS[L], UNITS[L]))
                    if x.back().exists(ns):
                        act.wait_ge(s_on[L], x.back().count(1, 1))
                    act.activation(o_raw[L][:, :], ps_o[0:OROWS, 0:ST], ACT.Copy).then_inc(s_oe[L], 1)

            def gelu(x, L, c):
                if x.exists(ns):
                    act.wait_ge(s_f1[L], x.count(HCH, c + 1))
                    if c == 0:
                        if x.back().exists(ns):
                            act.wait_ge(s_f2[L], x.back().count(1, 1))
                    act.activation(hid[L][:, c, :], ps_g[bank_of[f"f1_{c}_{L}"]][:, 0:ST], ACT.Gelu, bias=bfc1[L][:, c:c + 1])\
                       .then_inc(s_ge[L], 1)

            def keep(x):
                if x.exists(ns):
                    act.wait_ge(s_fin[0], x.count(1, 1))
                    if x.back().exists(ns):
                        act.wait_ge(s_xo[1], x.back().count(1, 1))
                    act.activation(x_keep[:, :, :], x_next[:, :, :], ACT.Copy).then_inc(s_keep, 1)

            def body(i):
                s0, s1, s2, s3 = Strip(i, 0), Strip(i, 1), Strip(i, 2), Strip(i, 3)
                probsT_out(s3, 1, 2)
                exps(s3, 1, 5)
                probsT_out(s3, 1, 3)
                probsT_out(s3, 1, 4)
                probsT_out(s3, 1, 5)
                o_out(s3, 1)
                turned(s2, "A1")
                exps(s1, 0, 0)
                probsT_out(s1, 0, 0)
                q_out(s2, 1)
                exps(s1, 0, 1)
                k_out(s2, 1)
                probsT_out(s1, 0, 1)
                o_out(s1, 0)
                turned(s3, "M1")
                gelu(s3, 1, 0)
                gelu(s3, 1, 1)
                gelu(s3, 1, 2)
                exps(s2, 1, 0)
                turned(s1, "M0")
                exps(s2, 1, 1)
                gelu(s1, 0, 0)
                gelu(s1, 0, 1)
                gelu(s1, 0, 2)
                probsT_out(s2, 1, 0)
                turned(s0, "A0")
                keep(s2)
                exps(s2, 1, 2)
                probsT_out(s2, 1, 1)
                exps(s2, 1, 3)
                q_out(s0, 0)
                k_out(s0, 0)
                exps(s2, 1, 4)

            iterate(act, body)

        @block.vector
        def _(dve):
            dve.memset(ones[:, :], 1.0).then_inc(s_memset, 1)
            dve.memset(mean_w[:, :], 1.0 / HID).then_inc(s_memset, 1)
            dve.memset(minus_half[:, :], -0.5).then_inc(s_memset, 1)
            dve.memset(ps_o[:, :], 0.0).then_inc(s_memset, 1)
            dve.wait_ge(s_memset, 4)
            dve.wait_ge(s_const, NCONST)
            step = [0]

            def done(ins, wait=True):
                step[0] += 1
                ins.then_inc(s_w, 1)
                if wait:
                    dve.wait_ge(s_w, step[0])

            for L in (0, 1):
                p = par96[L]
                dve.wait_ge(s_wps, L + 1)
                done(dve.tensor_tensor(bqkv[L][:, :], ps_g[L][0:C, 0:3], p[:, P96["bqkv"]:P96["bqkv"] + 3], ALU.add))
                done(dve.tensor_scalar(bqkv[L][:, 0:1], bqkv[L][:, 0:1], float(HD[L]) ** -0.5, None, ALU.mult))
            g3 = free(par128[0][:, P128["g3"]:P128["g3"] + 1], (1, HCH), (0, C))
            w2 = par128[0][:, P128["fc2"]:P128["fc2"] + HCH * C]
            done(dve.tensor_tensor(wg3[:, :].rearrange("p (n c) -> p n c", n=HCH), w2.rearrange("p (n c) -> p n c", n=HCH),
                                   g3, ALU.mult))
            done(dve.tensor_copy(wfc2[:, :, C:C + 1], free(mean_w[:, 0:1], (1, HCH), (1, 1))))
            done(dve.tensor_copy(hid_sq[:, :, 0:PT], free(par128[0][:, P128["b3"]:P128["b3"] + 1], (1, HCH), (0, PT))))
            for L in (0, 1):
                p = par96[L]
                done(dve.tensor_scalar(wqkv[L][:, :], p[:, P96["qkv"]:P96["qkv"] + 3 * C], p[:, P96["g1"]:P96["g1"] + 1],
                                       None, ALU.mult))
            for L in (0, 1):
                dve.wait_ge(s_wps, 3 + L)
                done(dve.tensor_tensor(brow[L][0:1, :], ps_s[L][0:1, 0:C], rows[L][0:1, 0:C], ALU.add))
            for L in (0, 1):
                p = par96[L]
                dve.tensor_scalar(wfc1[L][:, :], p[:, P96["fc1"]:P96["fc1"] + HID], p[:, P96["g2"]:P96["g2"] + 1],
                                  None, ALU.mult)
                dve.tensor_tensor(bfc1[L][:, :], ps_g[L][:, 3:3 + HCH], par128[L][:, P128["bfc1"]:P128["bfc1"] + HCH], ALU.add)
                done(dve.tensor_scalar(wqkv[L][:, 0:C], wqkv[L][:, 0:C], float(HD[L]) ** -0.5, None, ALU.mult))
            dve.wait_ge(s_wps, 5)
            dve.tensor_tensor(wfc2[:, :, 0:C], wg3[:, :].rearrange("p (n c) -> p n c", n=HCH),
                              free(ps_g[2][:, 0:1], (0, HCH), (1, C)), ALU.subtract)
            dve.wait_ge(s_wps, 6)
            for L in (0, 1):
                dve.tensor_copy(bfc2[L][:, :], ps_t[L][0:PT, 0:C])
            done(dve.tensor_copy(t_high[:, :], t_in[:, :]))
            dve.tensor_copy(tleft[:, :], tleft_in[:, :])
            done(dve.scalar_tensor_tensor(out=table[:, :], in0=t_high[:, :].bitcast(f32), scalar=tlow[:, 0:1], in1=t_in[:, :],
                                          op0=ALU.mult, op1=ALU.add))

            def stats(x, n, src, ready, ready_per):
                if not x.exists(ns):
                    return
                dve.wait_ge(ready, x.count(ready_per, ready_per))
                if x.back().exists(ns):
                    dve.wait_ge(s_xn[n], x.back().count(1, 1))
                for p in range(PAIRS):
                    ins = dve.bn_stats(bn[n][:, p, :], src[:, p, :])
                ins.then_inc(s_bn[n], 1)
                dve.wait_ge(s_bn[n], x.count(2, 1))
                dve.memset(gate[:, :], 0.0)
                for p in range(PAIRS):
                    ins = dve.bn_aggr(mv[n][:, p, :], bn[n][:, p, :])
                ins.then_inc(s_bn[n], 1)
                dve.wait_ge(s_bn[n], x.count(2, 2))
                dve.tensor_scalar(var_eps[n][:, :], free(mv[n][:, 0, 1:2], (2, PAIRS)), EPS, None, ALU.add)\
                   .then_inc(s_var[n], 1)

            def v_out(x, L, half):
                if not x.exists(ns):
                    return
                dve.wait_ge(s_v[L], x.count(2, half + 1))
                if x.back().exists(ns):
                    dve.wait_ge(s_pv[L], x.back().count(UNITS[L], UNITS[L]))
                g = ps_g[bank_of[("va", "vb")[half] + str(L)]][0:PT, 0:1]
                base = vM[L][:, 4 * half, 0, 0:1]
                if L == 0:
                    n = 2 * HD[0]
                    src, dst = free(g, (n, 8), (1, n)), free(base, (VW[0], 8), (1, n))
                    mask = free(vmask[:, 0:1], (0, 8), (1, n))
                else:
                    n = 2 * HD[1]
                    src = free(g, (3 * n, 8), (n, 3), (1, n))
                    dst = free(base, (3 * VW[1], 8), (VW[1] + n, 3), (1, n))
                    mask = free(vmask[:, 2 * HD[0]:2 * HD[0] + 1], (0, 8), (0, 3), (1, n))
                dve.tensor_tensor(dst, src, mask, ALU.mult).then_inc(s_vm[L], 1)

            def norm(x, n, src):
                if not x.exists(ns):
                    return
                dve.wait_ge(s_rstd[n], x.count(1, 1))
                if x.back().exists(ns):
                    dve.wait_ge(s_xt[n], x.back().count(1, 1))
                for p in range(PAIRS):
                    ins = dve.tensor_scalar(xn[n][:, p, :], src[:, p, :], mv[n][:, p, 0:1], rstd[n][:, p:p + 1],
                                            ALU.subtract, ALU.mult)
                ins.then_inc(s_xn[n], 1)

            def variants(x, L):
                if not x.exists(ns):
                    return
                dve.wait_ge(s_ke[L], x.count(1, 1))
                if x.back().exists(ns):
                    dve.wait_ge(s_s[L], x.back().count(UNITS[L], UNITS[L]))
                for m in range(4):
                    ins = dve.tensor_scalar(kM[L][:, m, :], kT[L][:, :], kmask[:, 4 * L + m:4 * L + m + 1], None, ALU.mult)
                ins.then_inc(s_km[L], 1)

            def shift(x, L, u):
                if not x.exists(ns):
                    return
                _, _, at = unit_place(L, u)
                dve.wait_ge(s_s[L], x.count(UNITS[L], u + 1))
                s = ps_s[at][0:SP, 0:8 * TOK].rearrange("p (h k) -> p h k", k=TOK)
                nm = negmax[at]
                dve.tensor_reduce(nm[:, :], s, AX.X, ALU.max, negate=True).then_inc(s_mx[L], 1)
                dve.wait_ge(s_mx[L], x.count(UNITS[L], u + 1))
                if free_from := before(x, SHIFTS, unit_over(s_ex), place, (L, u)):
                    dve.wait_ge(*free_from)
                dve.tensor_tensor(shifted[at][:, :].rearrange("p (h k) -> p h k", k=TOK), s,
                                  free(nm[:, 0:1], (1, 8), (0, TOK)), ALU.add).then_inc(s_sh[L], 1)

            def normalise(x, L):
                if x.exists(ns):
                    dve.wait_ge(s_sp[L], x.count(1, 1))
                    dve.reciprocal(o_rden[:, :], ps_g[bank_of[f"sp{L}"]][0:OROWS, 0:ST]).then_inc(s_rd[L], 1)
                    dve.wait_ge(s_rd[L], x.count(1, 1))
                    if x.back().exists(ns):
                        dve.wait_ge(s_pj[L], x.back().count(1, 1))
                    dve.tensor_tensor(o_norm[L][:, :], o_raw[L][:, :], o_rden[:, :], ALU.mult).then_inc(s_on[L], 1)

            def residual(x, L):
                if x.exists(ns):
                    dve.wait_ge(s_pj[L], x.count(1, 1))
                    if x.back().exists(ns):
                        dve.wait_ge(s_xb[L], x.back().count(1, 1))
                    if L == 1:
                        dve.wait_ge(s_keep, x.count(1, 1))
                    g = ps_g[bank_of[f"pj{L}"]][0:PT, 0:PAIRS * C].rearrange("p (n c) -> p n c", c=C)
                    dst, src = ((x_mid0, x_in), (x_mid1, x_keep))[L]
                    dve.tensor_tensor(dst[:, :, :], src[:, :, :], g, ALU.add).then_inc(s_xo[L], 1)

            def finish1(x):
                if x.exists(ns):
                    dve.wait_ge(s_f2[1], x.count(1, 1))
                    dve.wait_ge(s_xb[1], x.count(1, 1))
                    if x.back().exists(ns):
                        dve.wait_ge(s_store, x.back().count(16, 16))
                    g = ps_g[bank_of["f2_1"]][0:PT, 0:PAIRS * C].rearrange("p (n c) -> p n c", c=C)
                    dve.tensor_tensor(y_out[:, :, :], x_biased[1][:, :, :], g, ALU.add).then_inc(s_fin[1], 1)

            def third_stats(x):
                if not x.exists(ns):
                    return
                dve.wait_ge(s_f2[0], x.count(1, 1))
                g = ps_g[bank_of["f2_0"]]
                dve.tensor_copy(st3[:, :, :], free(g[0:PT, C:C + 1], (C + 2, PAIRS), (1, 2))).then_inc(s_v3, 1)
                dve.wait_ge(s_v3, x.count(4, 1))
                dve.scalar_tensor_tensor(out=var3[:, :], in0=st3[:, :, 0], scalar=-1.0, in1=st3[:, :, 0],
                                         op0=ALU.mult, op1=ALU.mult).then_inc(s_v3, 1)
                dve.wait_ge(s_v3, x.count(4, 2))
                dve.tensor_tensor(var3[:, :], var3[:, :], st3[:, :, 1], ALU.add).then_inc(s_v3, 1)
                dve.wait_ge(s_v3, x.count(4, 3))
                dve.tensor_scalar(var3[:, :], var3[:, :], 0.0, EPS, ALU.max, ALU.add).then_inc(s_v3, 1)

            def finish0(x):
                if not x.exists(ns):
                    return
                g = ps_g[bank_of["f2_0"]]
                dve.wait_ge(s_rstd3, x.count(1, 1))
                dve.wait_ge(s_xb[0], x.count(1, 1))
                if x.back().exists(ns):
                    dve.wait_ge(s_keep, x.back().count(1, 1))
                for p in range(PAIRS):
                    ins = dve.scalar_tensor_tensor(out=x_next[:, p, :], in0=g[0:PT, p * (C + 2):p * (C + 2) + C],
                                                   scalar=rstd3[:, p:p + 1], in1=x_biased[0][:, p, :],
                                                   op0=ALU.mult, op1=ALU.add)
                ins.then_inc(s_fin[0], 1)

            def body(i):
                s0, s1, s2, s3 = Strip(i, 0), Strip(i, 1), Strip(i, 2), Strip(i, 3)
                shift(s3, 1, 5)
                variants(s1, 0)
                third_stats(s2)
                v_out(s1, 0, 0)
                finish0(s2)
                stats(s2, "A1", x_next, s_fin[0], 1)
                shift(s1, 0, 0)
                norm(s2, "A1", x_next)
                v_out(s1, 0, 1)
                normalise(s3, 1)
                shift(s1, 0, 1)
                residual(s3, 1)
                stats(s3, "M1", x_mid1, s_xo[1], 1)
                variants(s2, 1)
                norm(s3, "M1", x_mid1)
                v_out(s2, 1, 0)
                normalise(s1, 0)
                shift(s2, 1, 0)
                residual(s1, 0)
                stats(s1, "M0", x_mid0, s_xo[0], 1)
                shift(s2, 1, 1)
                norm(s1, "M0", x_mid0)
                finish1(s3)
                stats(s0, "A0", x_in, s_load, 16)
                v_out(s2, 1, 1)
                shift(s2, 1, 2)
                norm(s0, "A0", x_in)
                shift(s2, 1, 3)
                shift(s2, 1, 4)

            iterate(dve, body)

        @block.gpsimd
        def _(pool):
            def inverse_root(x, n):
                if x.exists(ns):
                    pool.wait_ge(s_var[n], x.count(1, 1))
                    if x.back().exists(ns):
                        pool.wait_ge(s_xn[n], x.back().count(1, 1))
                    pool.tensor_tensor(rstd[n][:, :], var_eps[n][:, :], minus_half[:, :], ALU.pow).then_inc(s_rstd[n], 1)

            def add_bias(x, L, src):
                if x.exists(ns):
                    pool.wait_ge(s_xo[L], x.count(1, 1))
                    if x.back().exists(ns):
                        pool.wait_ge(s_fin[L], x.back().count(1, 1))
                    pool.tensor_tensor(x_biased[L][:, :, :], src[:, :, :], free(bfc2[L][:, 0:1], (0, PAIRS), (1, C)), ALU.add)\
                        .then_inc(s_xb[L], 1)

            def squares(x):
                if not x.exists(ns):
                    return
                pool.wait_ge(s_ge[0], x.count(HCH, HCH))
                if x.back().exists(ns):
                    pool.wait_ge(s_f2[0], x.back().count(1, 1))
                pool.tensor_tensor(hid_sq[:, :, :], hid[0][:, :, :], hid[0][:, :, :], ALU.mult).then_inc(s_sq, 1)
                pool.wait_ge(s_sq, x.count(3, 1))
                pool.tensor_tensor(hid_ss[:, :], hid_sq[:, 0, :], hid_sq[:, 1, :], ALU.add).then_inc(s_sq, 1)
                pool.wait_ge(s_sq, x.count(3, 2))
                pool.tensor_tensor(hid_ss[:, :], hid_ss[:, :], hid_sq[:, 2, :], ALU.add).then_inc(s_sq, 1)

            def rstd_of_third(x):
                if x.exists(ns):
                    pool.wait_ge(s_v3, x.count(4, 4))
                    if x.back().exists(ns):
                        pool.wait_ge(s_fin[0], x.back().count(1, 1))
                    pool.tensor_tensor(rstd3[:, :], var3[:, :], minus_half[:, :], ALU.pow).then_inc(s_rstd3, 1)

            def body(i):
                s0, s1, s2, s3 = Strip(i, 0), Strip(i, 1), Strip(i, 2), Strip(i, 3)
                rstd_of_third(s2)
                inverse_root(s2, "A1")
                inverse_root(s3, "M1")
                inverse_root(s1, "M0")
                add_bias(s3, 1, x_mid1)
                inverse_root(s0, "A0")
                squares(s1)
                add_bias(s1, 0, x_mid0)

            iterate(pool, body)


def _strips(x):
    x = np.roll(x, (-SHIFT, -SHIFT), axis=(1, 2))
    b = x.shape[0]
    x = x.reshape(b, 8, WS, PAIRS, 2, WS, C)
    return np.ascontiguousarray(x.transpose(1, 0, 4, 2, 5, 3, 6)).reshape(8 * b, PT, PAIRS * C)


def _image(y, b):
    y = y.reshape(8, b, 2, WS, WS, PAIRS, C).transpose(1, 0, 3, 5, 2, 4, 6).reshape(b, 8 * WS, 8 * WS, C)
    return np.ascontiguousarray(np.roll(y, (SHIFT, SHIFT), axis=(1, 2)))


def _table(t):
    c = np.stack(np.meshgrid(np.arange(WS), np.arange(WS), indexing="ij")).reshape(2, -1)
    rel = c[:, :, None] - c[:, None, :] + WS - 1
    return t[rel[0] * (2 * WS - 1) + rel[1]].transpose(0, 2, 1).reshape(TOK, -1)


def host_arrays(inp):
    a = {"x": _strips(inp["x"])}
    tab = np.concatenate([_table(inp["L0_conv_rpb_table"]), _table(inp["L1_conv_rel_bias_table"])], 1)
    a["tab"] = np.concatenate([tab, tab], 0)
    names = [dict(g1="ln1_g", b1="ln1_b", g2="ln2_g", b2="ln2_b", w1="fc1_w", c1="fc1_b", w2="fc2_w", c2="fc2_b"),
             dict(g1="norm1_w", b1="norm1_b", g2="norm2_w", b2="norm2_b", w1="mlp_w1", c1="mlp_b1", w2="mlp_w2", c2="mlp_b2")]
    for L in (0, 1):
        get = lambda n: inp[f"L{L}_conv_{names[L].get(n, n)}"]
        col = lambda v: v[:, None]
        a[f"par96_{L}"] = np.concatenate(
            [col(get("g1")), col(get("b1")), get("qkv_b").reshape(3, C).T, col(get("g2")), col(get("b2")),
             get("qkv_w"), get("w1"), get("proj_w")], 1)
        chunks = lambda v: v.reshape(HCH, 128).T
        norm3 = [chunks(get("ln3_g")), chunks(get("ln3_b"))] if L == 0 else [np.zeros((128, 2 * HCH), np.float32)]
        a[f"par128_{L}"] = np.concatenate(
            norm3 + [chunks(get("c1")), get("w2").reshape(HCH, 128, C).transpose(1, 0, 2).reshape(128, -1)], 1)
        a[f"rows{L}"] = np.concatenate([get("proj_b"), get("c2")])[None]
        w = np.zeros((OROWS, C), np.float32)
        w[0:TCH], w[64:64 + TCH] = get("proj_w")[:TCH], get("proj_w")[TCH:]
        a[f"wproj{L}"] = w
    a.update(shape_constants())
    return {n: np.ascontiguousarray(v) for n, v in a.items()}


def kernel(**inputs):
    import concourse.bacc as _bacc
    from concourse import mybir as _mybir
    from concourse.bass_utils import run_bass_kernel_spmd as _run

    arrays = host_arrays({n: np.asarray(v) for n, v in inputs.items()})
    nc = _bacc.Bacc("TRN2", target_bir_lowering=False, num_devices=1)
    d = {n: nc.dram_tensor(f"in_{n}", a.shape, _mybir.dt.from_np(a.dtype), kind="ExternalInput").ap()
         for n, a in arrays.items()}
    out = nc.dram_tensor("out_y", arrays["x"].shape, _mybir.dt.float32, kind="ExternalOutput").ap()
    swin_program(nc, d, out)
    r = _run(nc, [{f"in_{n}": a for n, a in arrays.items()}], core_ids=[0])
    return _image(np.asarray(r.results[0]["out_y"]), inputs["x"].shape[0])
```

```python
import concourse.bass as bass
from concourse import mybir
from contextlib import ExitStack
import numpy as np

LAST = 4
NSTRIP, ROWS_IN_IMAGE = 256, 8
WS, SHIFT = 7, 3
TOK = WS * WS
HALF = (0, 64)
SP = 64 + TOK
PAIRS = 4
PT = 2 * TOK
ST = PAIRS * PT
C, HID, HCH = 96, 384, 3
NH = (4, 12)
HD = (C // NH[0], C // NH[1])
UNITS = (NH[0] // 4 * 2, NH[1] // 4 * 2)
NHP = (NH[0] // 2, NH[1] // 2)
TCH = C // 2
VW = tuple(TCH + n // 2 for n in NH)
OROWS = 64 + max(VW)
ONE_ROW = max(VW)
EPS = 1e-5
UBUFS = 4
NREG = 6
BK = 2 * TOK + NREG


def _regions():
    r = (np.arange(WS) >= WS - SHIFT).astype(int)
    return np.repeat(r, WS), np.tile(r, WS)


def shape_constants():
    rr, rc = _regions()
    k = {}
    k["ident"] = np.eye(128, dtype=np.float32)
    c = np.arange(C)
    k["kmask"] = np.stack([(c // HD[0])[:, None] == np.arange(4), (c % 32 // HD[1])[:, None] == np.arange(4)], 1)\
        .reshape(C, 8).astype(np.float32)
    rep = (np.arange(PT) // TOK)[:, None]
    k["vmask"] = np.concatenate([(np.arange(2 * HD[L]) // HD[L])[None] == rep for L in (0, 1)], 1).astype(np.float32)
    for L in (0, 1):
        v = np.zeros((PT, 8, NHP[L], VW[L]), np.float32)
        for hp in range(NHP[L]):
            local = hp % (NHP[L] // 2)
            for r in (0, 1):
                v[r * TOK:(r + 1) * TOK, :, hp, TCH + 2 * local + r] = 1
        k[f"vinit{L}"] = v.reshape(PT, -1)
    left = np.zeros((BK, 2, SP), np.float32)
    for part in (0, 1):
        for h in HALF:
            left[part * TOK + np.arange(TOK), :, h + np.arange(TOK)] = 1
    for q in range(TOK):
        left[2 * TOK + rr[q], :, HALF[0] + q] = 1
        left[2 * TOK + rr[q], 0, HALF[1] + q] = 1
        left[2 * TOK + 2 + 2 * rr[q] + rc[q], 1, HALF[1] + q] = 1
    k["tleft"] = left.reshape(BK, -1)
    right = np.zeros((NREG, 2, sum(NH), TOK), np.float32)
    for g in (0, 1):
        right[g, 1] = -100.0 * (rr != g)
        for h in (0, 1):
            right[2 + 2 * g + h, 0] = -100.0 * (rc != h)
            right[2 + 2 * g + h, 1] = -100.0 * ((rr != g) | (rc != h))
    k["tmask"] = right.reshape(NREG, -1)
    k["tlow"] = -(np.arange(BK) // TOK == 1).astype(np.float32)[:, None]
    return k


class Strip:

    def __init__(self, i, off):
        self.i, self.off = i, off
        self.known = isinstance(i, int)

    def back(self, n=1):
        return Strip(self.i, self.off + n)

    def exists(self, n):
        return not self.known or 0 <= self.i - self.off < n

    def count(self, per, c):
        return (self.i - self.off) * per + c if self.known else self.i * per + (c - self.off * per)


def swin_program(nc, d, out, ns=NSTRIP, last_row_from=NSTRIP - NSTRIP // ROWS_IN_IMAGE):
    f32, f32r = mybir.dt.float32, mybir.dt.float32r
    ALU, ACT, AX = mybir.AluOpType, mybir.ActivationFunctionType, mybir.AxisListType
    ctx = ExitStack()
    with ctx:
        def sb(name, shape, dt=f32):
            return ctx.enter_context(nc.sbuf_tensor(name, shape, dt))

        def psum_bank(name, shape=(128, 512)):
            return ctx.enter_context(nc.psum_tensor(name, list(shape), f32))

        def sem(name):
            return ctx.enter_context(nc.semaphore(name))

        def free(ap, *dims):
            return bass.AP(ap.tensor, ap.offset, [list(ap.ap[0])] + [list(x) for x in dims])

        ident = sb("ident", [128, 128])
        kmask = sb("kmask", [C, 8])
        vmask = sb("vmask", [PT, 2 * HD[0] + 2 * HD[1]])
        tleft_in = sb("tleft_in", [BK, 2 * SP])
        tlow = sb("tlow", [BK, 1])
        NT = TOK * sum(NH)
        t_in = sb("t_in", [BK, 2 * NT])
        t_high = sb("t_high", [BK, 2 * NT], f32r)
        tleft = sb("tleft", [BK, 2 * SP], f32r)
        table = sb("table", [BK, 2 * NT], f32r)
        NP96 = 7 + 3 * C + HID + C
        par96 = [sb(f"par96_{L}", [C, NP96]) for L in (0, 1)]
        NP128 = 9 + HCH * C
        par128 = [sb(f"par128_{L}", [128, NP128]) for L in (0, 1)]
        rows = [sb(f"rows{L}", [1, 2 * C]) for L in (0, 1)]
        wqkv = [sb(f"wqkv{L}", [C, 3 * C]) for L in (0, 1)]
        bqkv = [sb(f"bqkv{L}", [C, 3]) for L in (0, 1)]
        wproj = [sb(f"wproj{L}", [OROWS, C]) for L in (0, 1)]
        brow = [sb(f"brow{L}", [1, C]) for L in (0, 1)]
        wfc1 = [sb(f"wfc1_{L}", [C, HID]) for L in (0, 1)]
        wfc1_high = [sb(f"wfc1_high{L}", [C, HID], f32r) for L in (0, 1)]
        wfc1_low = [sb(f"wfc1_low{L}", [C, HID], f32r) for L in (0, 1)]
        bfc1 = [sb(f"bfc1_{L}", [128, HCH]) for L in (0, 1)]
        wg3 = sb("wg3", [128, HCH * C])
        wfc2 = sb("wfc2", [128, HCH, C + 1])
        ones = sb("ones", [128, 128])
        mean_w = sb("mean_w", [128, 128])
        bfc2 = [sb(f"bfc2_{L}", [PT, C]) for L in (0, 1)]

        x_in = sb("x_in", [PT, PAIRS, C])
        x_mid0 = sb("x_mid0", [PT, PAIRS, C])
        x_next = sb("x_next", [PT, PAIRS, C])
        x_keep = sb("x_keep", [PT, PAIRS, C])
        x_mid1 = sb("x_mid1", [PT, PAIRS, C])
        x_biased = [sb(f"x_biased{L}", [PT, PAIRS, C]) for L in (0, 1)]
        y_out = sb("y_out", [PT, PAIRS, C])
        LN = ("A0", "M0", "A1", "M1")
        bn = {n: sb("bn" + n, [PT, PAIRS, 6]) for n in LN}
        mv = {n: sb("mv" + n, [PT, PAIRS, 2]) for n in LN}
        var_eps = {n: sb("var_eps" + n, [PT, PAIRS]) for n in LN}
        gate = sb("gate", [1, 1])
        minus_half = sb("minus_half", [PT, PAIRS])
        rstd = {n: sb("rstd" + n, [PT, PAIRS]) for n in LN}
        xn = {n: sb("xn" + n, [PT, PAIRS, C]) for n in LN}
        xnT_a = [sb(f"xnT_a{L}", [C, 8, 2, TOK]) for L in (0, 1)]
        xnT_high = [sb(f"xnT_high{L}", [C, ST], f32r) for L in (0, 1)]
        xnT_low = [sb(f"xnT_low{L}", [C, ST], f32r) for L in (0, 1)]
        qT = [sb(f"qT{L}", [C, ST]) for L in (0, 1)]
        kT = [sb(f"kT{L}", [C, ST]) for L in (0, 1)]
        kM = [sb(f"kM{L}", [C, 4, ST]) for L in (0, 1)]
        vM = [sb(f"vM{L}", [PT, 8, NHP[L], VW[L]]) for L in (0, 1)]
        negmax = [sb(f"negmax{n}", [SP, 8]) for n in range(UBUFS)]
        shifted = [sb(f"shifted{n}", [SP, 2 * 4 * TOK]) for n in range(UBUFS)]
        probs = [sb(f"probs{n}", [SP, 2 * 4 * TOK]) for n in range(UBUFS)]
        probsT = [sb(f"probsT{n}", [PT, 4, 2, TOK]) for n in range(UBUFS)]
        o_raw = [sb(f"o_raw{L}", [OROWS, ST]) for L in (0, 1)]
        rden = [sb(f"rden{L}", [PT, 2 * PAIRS, NH[L] // 2]) for L in (0, 1)]
        wide = [sb(f"wide{L}", [PT, PAIRS, 128]) for L in (0, 1)]
        o_norm = [sb(f"o_norm{L}", [OROWS, ST]) for L in (0, 1)]
        hid = [sb(f"hid{L}", [128, HCH, ST]) for L in (0, 1)]
        hid_sq = sb("hid_sq", [128, HCH, ST])
        hid_ss = sb("hid_ss", [128, ST])
        st3 = sb("st3", [PT, PAIRS, 2])
        var3 = sb("var3", [PT, PAIRS])
        rstd3 = sb("rstd3", [PT, PAIRS])

        ps_o = psum_bank("ps_o")
        ps = [psum_bank(f"ps{n}") for n in range(7)]

        s_const = sem("s_const")
        s_memset = sem("s_memset")
        s_w = sem("s_w")
        s_wps = sem("s_wps")
        s_brow = sem("s_brow")
        s_load = sem("s_load")
        s_store = sem("s_store")
        s_bn = {n: sem("s_bn" + n) for n in LN}
        s_var = {n: sem("s_var" + n) for n in LN}
        s_rstd = {n: sem("s_rstd" + n) for n in LN}
        s_xn = {n: sem("s_xn" + n) for n in LN}
        s_xt = {n: sem("s_xt" + n) for n in LN}
        s_xe = {n: sem("s_xe" + n) for n in LN}
        pairsem = lambda name: [sem(f"{name}{L}") for L in (0, 1)]
        s_xl = pairsem("s_xl")
        s_q, s_qe = pairsem("s_q"), pairsem("s_qe")
        s_k, s_ke = pairsem("s_k"), pairsem("s_ke")
        s_km = pairsem("s_km")
        s_v, s_vm = pairsem("s_v"), pairsem("s_vm")
        s_s = pairsem("s_s")
        s_mx = pairsem("s_mx")
        s_sh = pairsem("s_sh")
        s_ex = pairsem("s_ex")
        s_pt, s_pe = pairsem("s_pt"), pairsem("s_pe")
        s_pv = pairsem("s_pv")
        s_oe = pairsem("s_oe")
        s_dt = pairsem("s_dt")
        s_rd = pairsem("s_rd")
        s_wd = pairsem("s_wd")
        s_sp = pairsem("s_sp")
        s_on = pairsem("s_on")
        s_pj = pairsem("s_pj")
        s_xo = pairsem("s_xo")
        s_xb = pairsem("s_xb")
        s_f1, s_ge = pairsem("s_f1"), pairsem("s_ge")
        s_sq = sem("s_sq")
        s_f2 = pairsem("s_f2")
        s_v3 = sem("s_v3")
        s_rstd3 = sem("s_rstd3")
        s_fin = pairsem("s_fin")
        s_keep = sem("s_keep")

        BANKS = [("sc14", 3, 1), ("sc15", 3, 2), ("xtA0", 1, 4), ("T12", 3, 6), ("T13", 3, 0), ("q0", 1, 5), ("T14", 3, 2),
                 ("k0", 1, 3), ("f2_0", 2, 6), ("sc00", 1, 4), ("T15", 3, 2), ("va0", 1, 6), ("dt1", 3, 2), ("sc01", 1, 3),
                 ("vb0", 1, 1), ("sp1", 3, 0), ("xtA1", 2, 4), ("pj1", 3, 2), ("q1", 2, 4), ("k1", 2, 5), ("T00", 1, 2),
                 ("T01", 1, 1), ("va1", 2, 6), ("sc10", 2, 3), ("dt0", 1, 0), ("xtM1", 3, 1), ("sc11", 2, 2), ("sp0", 1, 4),
                 ("sc12", 2, 5), ("pj0", 1, 4), ("f1_0_1", 3, 6), ("T10", 2, 4), ("f1_1_1", 3, 0), ("f1_2_1", 3, 2),
                 ("vb1", 2, 3), ("sc13", 2, 6), ("T11", 2, 0), ("xtM0", 1, 2), ("f2_1", 3, 5), ("f1_0_0", 1, 4),
                 ("f1_1_0", 1, 1), ("f1_2_0", 1, 3)]
        bank_of = {use: n for use, _, n in BANKS}
        G = [(use, lag) for use, lag, _ in BANKS]
        O = [(0, 1), (1, 2)]
        SHIFTS = [((1, 4), 3), ((1, 5), 3), ((0, 0), 1), ((0, 1), 1), ((1, 0), 2), ((1, 1), 2), ((1, 2), 2), ((1, 3), 2)]
        EXPS = [((1, 2), 3), ((1, 3), 3), ((1, 4), 3), ((1, 5), 3), ((0, 0), 1), ((0, 1), 1), ((1, 0), 2), ((1, 1), 2)]
        COPIES = [((1, 2), 3), ((1, 3), 3), ((1, 4), 3), ((1, 5), 3), ((0, 0), 1), ((0, 1), 1), ((1, 0), 2), ((1, 1), 2)]
        buffer = lambda use: [unit for unit, _ in SHIFTS].index(use) % UBUFS

        over_g = {}
        for n in LN:
            over_g["xt" + n] = (s_xe[n], 1, 1) if n[0] == "A" else (s_xl[int(n[1])], 1, 1)
        for L in (0, 1):
            over_g[f"q{L}"] = (s_qe[L], 1, 1)
            over_g[f"k{L}"] = (s_ke[L], 1, 1)
            over_g[f"va{L}"] = (s_vm[L], 2, 1)
            over_g[f"vb{L}"] = (s_vm[L], 2, 2)
            over_g[f"dt{L}"] = (s_rd[L], 1, 1)
            over_g[f"sp{L}"] = (s_on[L], 1, 1)
            over_g[f"pj{L}"] = (s_xo[L], 1, 1)
            over_g[f"f2_{L}"] = (s_fin[L], 1, 1)
            for c in range(HCH):
                over_g[f"f1_{c}_{L}"] = (s_ge[L], HCH, c + 1)
            for u in range(UNITS[L]):
                over_g[f"sc{L}{u}"] = (s_sh[L], UNITS[L], u + 1)
                over_g[f"T{L}{u}"] = (s_pe[L], UNITS[L], u + 1)
        unit_over = lambda s: {(L, u): (s[L], UNITS[L], u + 1) for (L, u), _ in SHIFTS}

        def before(x, ring, over, slot, use):
            at = [n for n, _ in ring].index(use)
            assert ring[at][1] == x.off
            wraps = 0
            for _ in range(4 * len(ring)):
                at -= 1
                if at < 0:
                    at, wraps = at + len(ring), wraps + 1
                other, lag = ring[at]
                y = Strip(x.i, lag + wraps)
                if slot(other) == slot(use) and y.exists(ns):
                    semaphore, per, c = over[other]
                    return semaphore, y.count(per, c)
            return None

        def g_before(x, use):
            return before(x, G, over_g, lambda n: bank_of[n], use)

        def unit_place(L, u):
            return u // (UNITS[L] // 2), u % (UNITS[L] // 2), buffer((L, u))

        NCONST = 0
        loads = [(ident[:, :], d["ident"]), (kmask[:, :], d["kmask"]), (vmask[:, :], d["vmask"]),
                 (tleft_in[:, :], d["tleft"]), (tlow[:, :], d["tlow"]),
                 (t_in[2 * TOK:BK, :], d["tmask"])]
        for v in (0, 1):
            loads.append((t_in[0:2 * TOK, v * NT:(v + 1) * NT], d["tab"]))
        for L in (0, 1):
            loads += [(par96[L][:, :], d[f"par96_{L}"]),
                      (par128[L][:, :], d[f"par128_{L}"]), (rows[L][:, :], d[f"rows{L}"]),
                      (wproj[L][:, :], d[f"wproj{L}"]),
                      (vM[L][:, :, :, :].rearrange("p w h c -> p (w h c)"), d[f"vinit{L}"])]
        NCONST = 16 * len(loads)
        P96 = {"g1": 0, "b1": 1, "bqkv": 2, "g2": 5, "b2": 6, "qkv": 7, "fc1": 7 + 3 * C, "proj": 7 + 3 * C + HID}
        P128 = {"g3": 0, "b3": 3, "bfc1": 6, "fc2": 9}

        def iterate(eng, body):
            total, first = ns + LAST, LAST + 2
            for i in range(min(first, total)):
                body(i)
            if ns > first:
                with eng.Fori(first, ns) as i:
                    body(i)
            for i in range(max(first, ns), total):
                body(i)

        block = ctx.enter_context(nc.Block())

        @block.sync
        def _(sp):
            for dst, src in loads:
                sp.dma_start(dst, src).then_inc(s_const, 16)
            for L in (0, 1):
                sp.wait_ge(s_w, 10 + L)
                sp.dma_start(wproj[L][ONE_ROW:ONE_ROW + 1, :], brow[L][0:1, :]).then_inc(s_brow, 16)

            def body(i):
                a0 = Strip(i, 0)
                if a0.exists(ns):
                    if a0.back().exists(ns):
                        sp.wait_ge(s_xo[0], a0.back().count(1, 1))
                    n = i if isinstance(i, int) else bass.ds(i, 1)
                    src = d["x"][n, :, :] if isinstance(i, int) else d["x"][n, :, :].rearrange("a p c -> (a p) c")
                    sp.dma_start(x_in[:, :, :].rearrange("p a c -> p (a c)"), src).then_inc(s_load, 16)
                m1 = Strip(i, 4)
                if m1.exists(ns):
                    sp.wait_ge(s_fin[1], m1.count(1, 1))
                    if isinstance(i, int):
                        dst = out[i - 4, :, :]
                    else:
                        dst = out[bass.ds(i - 4, 1), :, :].rearrange("a p c -> (a p) c")
                    sp.dma_start(dst, y_out[:, :, :].rearrange("p a c -> p (a c)")).then_inc(s_store, 16)

            iterate(sp, body)
            sp.wait_ge(s_store, 16 * ns)

        @block.tensor
        def _(pe):
            pe.wait_ge(s_const, NCONST)
            pe.wait_ge(s_memset, 6)
            for L in (0, 1):
                p = par96[L]
                for n in range(3):
                    pe.matmul(ps[L][0:C, n:n + 1], p[:, P96["qkv"] + C * n:P96["qkv"] + C * (n + 1)],
                              p[:, P96["b1"]:P96["b1"] + 1], start=True, stop=True)
                for n in range(HCH):
                    mm = pe.matmul(ps[L][:, 3 + n:4 + n], p[:, P96["fc1"] + 128 * n:P96["fc1"] + 128 * (n + 1)],
                                   p[:, P96["b2"]:P96["b2"] + 1], start=True, stop=True)
                mm.then_inc(s_wps, 1)
            for L in (0, 1):
                pe.wait_ge(s_w, 2 + 2 * L)
                pe.matmul(ps[3 + L][0:1, 0:C], bqkv[L][:, 2:3], par96[L][:, P96["proj"]:P96["proj"] + C],
                          start=True, stop=True).then_inc(s_wps, 1)
            pe.wait_ge(s_w, 6)
            for c in range(HCH):
                mm = pe.matmul(ps[2][:, 0:C], mean_w[:, :], wg3[:, C * c:C * (c + 1)], start=(c == 0), stop=(c == HCH - 1))
            mm.then_inc(s_wps, 1)
            pe.wait_ge(s_w, 7)
            for c in range(HCH):
                pe.matmul(ps[5][0:PT, 0:C], hid_sq[:, c, 0:PT], par128[0][:, P128["fc2"] + C * c:P128["fc2"] + C * (c + 1)],
                          start=(c == 0), stop=False)
            pe.matmul(ps[5][0:PT, 0:C], ones[0:1, 0:PT], rows[0][0:1, C:2 * C], start=False, stop=True)
            pe.matmul(ps[6][0:PT, 0:C], ones[0:1, 0:PT], rows[1][0:1, C:2 * C], start=True, stop=True).then_inc(s_wps, 1)
            pe.wait_ge(s_w, 19)
            pe.wait_ge(s_brow, 32)

            def xT(x, n):
                if x.exists(ns):
                    pe.wait_ge(s_xn[n], x.count(1, 1))
                    use = "xt" + n
                    if free_from := g_before(x, use):
                        pe.wait_ge(*free_from)
                    g = ps[bank_of[use]]
                    for p in range(PAIRS):
                        mm = pe.transpose(g[0:C, p * PT:(p + 1) * PT], xn[n][:, p, :], ident[0:PT, 0:PT])
                    mm.then_inc(s_xt[n], 1)

            def qk(x, L, name, part, signal):
                if x.exists(ns):
                    pe.wait_ge(s_xe[f"A{L}"], x.count(1, 1))
                    use = f"{name}{L}"
                    if free_from := g_before(x, use):
                        pe.wait_ge(*free_from)
                    g = ps[bank_of[use]]
                    pe.matmul(g[0:C, 0:ST], wqkv[L][:, part * C:(part + 1) * C], xnT_a[L][:, :, 0, :], start=True, stop=True)\
                      .then_inc(signal[L], 1)

            def v(x, L, half):
                if x.exists(ns):
                    pe.wait_ge(s_xe[f"A{L}"], x.count(1, 1))
                    use = ("va", "vb")[half] + str(L)
                    if free_from := g_before(x, use):
                        pe.wait_ge(*free_from)
                    g = ps[bank_of[use]]
                    for n in range(4):
                        w = 4 * half + n
                        twice = xnT_a[L][:, w, :, :].rearrange("p r t -> p (r t)")
                        mm = pe.matmul(g[0:PT, n * C:(n + 1) * C], twice, wqkv[L][:, 2 * C:3 * C], start=True, stop=True)
                    mm.then_inc(s_v[L], 1)

            def scores(x, L, u):
                if not x.exists(ns):
                    return
                two_pairs, group, buf = unit_place(L, u)
                if free_from := g_before(x, f"sc{L}{u}"):
                    pe.wait_ge(*free_from)
                s = ps[bank_of[f"sc{L}{u}"]]
                pe.wait_ge(s_qe[L], x.count(1, 1))
                pe.wait_ge(s_km[L], x.count(1, 1))
                col = TOK * (4 * group + (NH[0] if L else 0))
                if x.known:
                    start = (1 if x.i - x.off >= last_row_from else 0) * NT + col
                    tab = table[:, start:start + 4 * TOK]
                else:
                    which = (x.i + (256 - last_row_from - x.off)) // 256
                    tab = table[:, bass.ds(which * NT + col, 4 * TOK)]
                for p in (0, 1):
                    left = 1 if 2 * two_pairs + p == PAIRS - 1 else 0
                    pe.matmul(s[0:SP, 4 * TOK * p:4 * TOK * (p + 1)], tleft[:, left * SP:(left + 1) * SP], tab,
                              start=(p == 0), stop=False, skip_group_check=True)
                r = slice(0, C) if L == 0 else slice(32 * group, 32 * group + 32)
                for p in (0, 1):
                    for h in (0, 1):
                        t = (2 * two_pairs + p) * PT + h * TOK
                        mm = pe.matmul(s[HALF[h]:HALF[h] + TOK, 4 * TOK * p:4 * TOK * (p + 1)], qT[L][r, t:t + TOK],
                                       kM[L][r, :, t:t + TOK], start=False, stop=True, skip_group_check=True)
                mm.then_inc(s_s[L], 1)

            def probs_turn(x, L, u):
                if not x.exists(ns):
                    return
                _, _, buf = unit_place(L, u)
                pe.wait_ge(s_ex[L], x.count(UNITS[L], u + 1))
                if free_from := g_before(x, f"T{L}{u}"):
                    pe.wait_ge(*free_from)
                for n in range(4):
                    mm = pe.transpose(ps[bank_of[f"T{L}{u}"]][0:PT, n * SP:(n + 1) * SP], probs[buf][:, n * PT:(n + 1) * PT],
                                      ident[0:SP, 0:SP])
                mm.then_inc(s_pt[L], 1)

            def attend(x, L, u):
                if not x.exists(ns):
                    return
                two_pairs, group, buf = unit_place(L, u)
                pe.wait_ge(s_pe[L], x.count(UNITS[L], u + 1))
                pe.wait_ge(s_vm[L], x.count(2, 2))
                if u == 0:
                    if free_from := before(x, O, {0: (s_oe[0], 1, 1), 1: (s_oe[1], 1, 1)}, lambda n: 0, L):
                        pe.wait_ge(*free_from)
                begun = set()
                for p in (0, 1):
                    for h in (0, 1):
                        w = 2 * (2 * two_pairs + p) + h
                        for n in (0, 1):
                            hp = 2 * group + n
                            tile = hp // (NHP[L] // 2)
                            first = u == {(0, 0): 0, (0, 1): 0, (1, 0): 0, (1, 1): 1}[L, tile] and tile not in begun
                            begun.add(tile)
                            mm = pe.matmul(ps_o[64 * tile:64 * tile + VW[L], w * TOK:(w + 1) * TOK], vM[L][:, w, hp, :],
                                           probsT[buf][:, 2 * p + n, h, :], start=first, stop=True, skip_group_check=True)
                mm.then_inc(s_pv[L], 1)

            def turn_den(x, L):
                if x.exists(ns):
                    pe.wait_ge(s_oe[L], x.count(1, 1))
                    use = f"dt{L}"
                    if free_from := g_before(x, use):
                        pe.wait_ge(*free_from)
                    g = ps[bank_of[use]]
                    for p in range(PAIRS):
                        mm = pe.transpose(g[0:PT, p * OROWS:(p + 1) * OROWS], o_raw[L][:, p * PT:(p + 1) * PT],
                                          ident[0:OROWS, 0:OROWS])
                    mm.then_inc(s_dt[L], 1)

            def spread_den(x, L):
                if x.exists(ns):
                    pe.wait_ge(s_wd[L], x.count(1, 1))
                    use = f"sp{L}"
                    if free_from := g_before(x, use):
                        pe.wait_ge(*free_from)
                    g = ps[bank_of[use]]
                    for p in range(PAIRS):
                        mm = pe.transpose(g[0:OROWS, p * PT:(p + 1) * PT], wide[L][:, p, 0:OROWS], ident[0:PT, 0:PT])
                    mm.then_inc(s_sp[L], 1)

            def project(x, L):
                if x.exists(ns):
                    pe.wait_ge(s_on[L], x.count(1, 1))
                    use = f"pj{L}"
                    if free_from := g_before(x, use):
                        pe.wait_ge(*free_from)
                    g = ps[bank_of[use]]
                    for p in range(PAIRS):
                        mm = pe.matmul(g[0:PT, p * C:(p + 1) * C], o_norm[L][:, p * PT:(p + 1) * PT], wproj[L][:, :],
                                       start=True, stop=True)
                    mm.then_inc(s_pj[L], 1)

            def fc1(x, L, c):
                if x.exists(ns):
                    pe.wait_ge(s_xe[f"M{L}"], x.count(1, 1))
                    use = f"f1_{c}_{L}"
                    if free_from := g_before(x, use):
                        pe.wait_ge(*free_from)
                    g = ps[bank_of[use]]
                    w = slice(128 * c, 128 * (c + 1))
                    pe.matmul(g[:, 0:ST], wfc1_high[L][:, w], xnT_high[L][:, :], start=True, stop=False)
                    pe.matmul(g[:, 0:ST], wfc1_low[L][:, w], xnT_high[L][:, :], start=False, stop=False)
                    pe.wait_ge(s_xl[L], x.count(1, 1))
                    pe.matmul(g[:, 0:ST], wfc1_high[L][:, w], xnT_low[L][:, :], start=False, stop=True)\
                      .then_inc(s_f1[L], 1)

            def fc2(x, L):
                if not x.exists(ns):
                    return
                pe.wait_ge(s_ge[L], x.count(HCH, HCH))
                if L == 0:
                    pe.wait_ge(s_sq, x.count(3, 3))
                use = f"f2_{L}"
                if free_from := g_before(x, use):
                    pe.wait_ge(*free_from)
                g = ps[bank_of[use]]
                step, width = (C + 2, C + 1) if L == 0 else (C, C)
                for p in range(PAIRS):
                    t = slice(p * PT, (p + 1) * PT)
                    for c in range(HCH):
                        w = wfc2[:, c, :] if L == 0 else par128[1][:, P128["fc2"] + C * c:P128["fc2"] + C * (c + 1)]
                        mm = pe.matmul(g[0:PT, p * step:p * step + width], hid[L][:, c, t], w, start=(c == 0), stop=(c == HCH - 1))
                    if L == 0:
                        mm = pe.matmul(g[0:PT, p * step + C + 1:(p + 1) * step], hid_ss[:, t], mean_w[:, 0:1],
                                       start=True, stop=True)
                mm.then_inc(s_f2[L], 1)

            def body(i):
                s1, s2, s3 = Strip(i, 1), Strip(i, 2), Strip(i, 3)
                scores(s3, 1, 4)
                scores(s3, 1, 5)
                xT(s1, "A0")
                attend(s3, 1, 1)
                probs_turn(s3, 1, 2)
                probs_turn(s3, 1, 3)
                qk(s1, 0, "q", 0, s_q)
                probs_turn(s3, 1, 4)
                qk(s1, 0, "k", 1, s_k)
                fc2(s2, 0)
                scores(s1, 0, 0)
                attend(s3, 1, 2)
                probs_turn(s3, 1, 5)
                attend(s3, 1, 3)
                attend(s3, 1, 4)
                attend(s3, 1, 5)
                v(s1, 0, 0)
                turn_den(s3, 1)
                scores(s1, 0, 1)
                v(s1, 0, 1)
                spread_den(s3, 1)
                xT(s2, "A1")
                project(s3, 1)
                qk(s2, 1, "q", 0, s_q)
                qk(s2, 1, "k", 1, s_k)
                probs_turn(s1, 0, 0)
                probs_turn(s1, 0, 1)
                v(s2, 1, 0)
                attend(s1, 0, 0)
                attend(s1, 0, 1)
                scores(s2, 1, 0)
                turn_den(s1, 0)
                xT(s3, "M1")
                scores(s2, 1, 1)
                spread_den(s1, 0)
                scores(s2, 1, 2)
                project(s1, 0)
                fc1(s3, 1, 0)
                probs_turn(s2, 1, 0)
                fc1(s3, 1, 1)
                fc1(s3, 1, 2)
                v(s2, 1, 1)
                scores(s2, 1, 3)
                probs_turn(s2, 1, 1)
                xT(s1, "M0")
                fc2(s3, 1)
                fc1(s1, 0, 0)
                fc1(s1, 0, 1)
                fc1(s1, 0, 2)
                attend(s2, 1, 0)

            iterate(pe, body)

        @block.scalar
        def _(act):
            def turned(x, n):
                if not x.exists(ns):
                    return
                act.wait_ge(s_xt[n], x.count(1, 1))
                a = n[0] == "A"
                L = int(n[1])
                if x.back().exists(ns):
                    if a:
                        act.wait_ge(s_v[L], x.back().count(2, 2))
                    else:
                        act.wait_ge(s_f1[L], x.back().count(HCH, HCH))
                g = ps[bank_of["xt" + n]]
                if a:
                    dst, src = xnT_a[L][:, :, :, :], free(g[0:C, 0:1], (TOK, 8), (0, 2), (1, TOK))
                else:
                    dst, src = xnT_high[L][:, :], g[0:C, 0:ST]
                act.activation(dst, src, ACT.Copy).then_inc(s_xe[n], 1)

            def q_out(x, L):
                if x.exists(ns):
                    act.wait_ge(s_q[L], x.count(1, 1))
                    if x.back().exists(ns):
                        act.wait_ge(s_s[L], x.back().count(UNITS[L], UNITS[L]))
                    act.activation(qT[L][:, :], ps[bank_of[f"q{L}"]][0:C, 0:ST], ACT.Identity, bias=bqkv[L][:, 0:1])\
                       .then_inc(s_qe[L], 1)

            def k_out(x, L):
                if x.exists(ns):
                    act.wait_ge(s_k[L], x.count(1, 1))
                    if x.back().exists(ns):
                        act.wait_ge(s_km[L], x.back().count(1, 1))
                    act.activation(kT[L][:, :], ps[bank_of[f"k{L}"]][0:C, 0:ST], ACT.Identity, bias=bqkv[L][:, 1:2])\
                       .then_inc(s_ke[L], 1)

            def exps(x, L, u):
                if x.exists(ns):
                    _, _, buf = unit_place(L, u)
                    act.wait_ge(s_sh[L], x.count(UNITS[L], u + 1))
                    if free_from := before(x, EXPS, unit_over(s_pt), buffer, (L, u)):
                        act.wait_ge(*free_from)
                    act.activation(probs[buf][:, :], shifted[buf][:, :], ACT.Exp).then_inc(s_ex[L], 1)

            def probsT_out(x, L, u):
                if x.exists(ns):
                    _, _, buf = unit_place(L, u)
                    act.wait_ge(s_pt[L], x.count(UNITS[L], u + 1))
                    if free_from := before(x, COPIES, unit_over(s_pv), buffer, (L, u)):
                        act.wait_ge(*free_from)
                    act.activation(probsT[buf][:, :, :, :], free(ps[bank_of[f"T{L}{u}"]][0:PT, 0:1], (SP, 4), (64, 2), (1, TOK)),
                                   ACT.Copy).then_inc(s_pe[L], 1)

            def o_out(x, L):
                if x.exists(ns):
                    act.wait_ge(s_pv[L], x.count(UNITS[L], UNITS[L]))
                    if x.back().exists(ns):
                        act.wait_ge(s_on[L], x.back().count(1, 1))
                    act.activation(o_raw[L][:, :], ps_o[0:OROWS, 0:ST], ACT.Copy).then_inc(s_oe[L], 1)

            def widen_den(x, L):
                if x.exists(ns):
                    act.wait_ge(s_rd[L], x.count(1, 1))
                    if x.back().exists(ns):
                        act.wait_ge(s_sp[L], x.back().count(1, 1))
                    act.activation(free(wide[L][:, 0, 0:1], (64, 2 * PAIRS), (HD[L], NH[L] // 2), (1, HD[L])),
                                   free(rden[L][:, 0, 0:1], (NH[L] // 2, 2 * PAIRS), (1, NH[L] // 2), (0, HD[L])),
                                   ACT.Copy).then_inc(s_wd[L], 1)

            def gelu(x, L, c):
                if x.exists(ns):
                    act.wait_ge(s_f1[L], x.count(HCH, c + 1))
                    if c == 0:
                        if x.back().exists(ns):
                            act.wait_ge(s_f2[L], x.back().count(1, 1))
                    act.activation(hid[L][:, c, :], ps[bank_of[f"f1_{c}_{L}"]][:, 0:ST], ACT.Gelu, bias=bfc1[L][:, c:c + 1])\
                       .then_inc(s_ge[L], 1)

            def keep(x):
                if x.exists(ns):
                    act.wait_ge(s_fin[0], x.count(1, 1))
                    if x.back().exists(ns):
                        act.wait_ge(s_xo[1], x.back().count(1, 1))
                    act.activation(x_keep[:, :, :], x_next[:, :, :], ACT.Copy).then_inc(s_keep, 1)

            def body(i):
                s1, s2, s3 = Strip(i, 1), Strip(i, 2), Strip(i, 3)
                exps(s3, 1, 2)
                exps(s3, 1, 3)
                turned(s1, "A0")
                exps(s3, 1, 4)
                probsT_out(s3, 1, 2)
                exps(s3, 1, 5)
                probsT_out(s3, 1, 3)
                q_out(s1, 0)
                probsT_out(s3, 1, 4)
                k_out(s1, 0)
                probsT_out(s3, 1, 5)
                o_out(s3, 1)
                widen_den(s3, 1)
                exps(s1, 0, 0)
                turned(s2, "A1")
                exps(s1, 0, 1)
                k_out(s2, 1)
                probsT_out(s1, 0, 0)
                probsT_out(s1, 0, 1)
                q_out(s2, 1)
                o_out(s1, 0)
                widen_den(s1, 0)
                turned(s3, "M1")
                keep(s2)
                exps(s2, 1, 0)
                exps(s2, 1, 1)
                gelu(s3, 1, 0)
                gelu(s3, 1, 1)
                gelu(s3, 1, 2)
                probsT_out(s2, 1, 0)
                turned(s1, "M0")
                probsT_out(s2, 1, 1)
                gelu(s1, 0, 0)
                gelu(s1, 0, 1)
                gelu(s1, 0, 2)

            iterate(act, body)

        @block.vector
        def _(dve):
            dve.memset(ones[:, :], 1.0).then_inc(s_memset, 1)
            dve.memset(mean_w[:, :], 1.0 / HID).then_inc(s_memset, 1)
            dve.memset(minus_half[:, :], -0.5).then_inc(s_memset, 1)
            dve.memset(ps_o[:, :], 1.0).then_inc(s_memset, 1)
            for L in (0, 1):
                dve.memset(wide[L][:, :, :], 1.0).then_inc(s_memset, 1)
            dve.wait_ge(s_memset, 6)
            dve.wait_ge(s_const, NCONST)
            step = [0]

            def done(ins, wait=True):
                step[0] += 1
                ins.then_inc(s_w, 1)
                if wait:
                    dve.wait_ge(s_w, step[0])

            for L in (0, 1):
                p = par96[L]
                dve.wait_ge(s_wps, L + 1)
                done(dve.tensor_tensor(bqkv[L][:, :], ps[L][0:C, 0:3], p[:, P96["bqkv"]:P96["bqkv"] + 3], ALU.add))
                done(dve.tensor_scalar(bqkv[L][:, 0:1], bqkv[L][:, 0:1], float(HD[L]) ** -0.5, None, ALU.mult))
            g3 = free(par128[0][:, P128["g3"]:P128["g3"] + 1], (1, HCH), (0, C))
            w2 = par128[0][:, P128["fc2"]:P128["fc2"] + HCH * C]
            done(dve.tensor_tensor(wg3[:, :].rearrange("p (n c) -> p n c", n=HCH), w2.rearrange("p (n c) -> p n c", n=HCH),
                                   g3, ALU.mult))
            done(dve.tensor_copy(wfc2[:, :, C:C + 1], free(mean_w[:, 0:1], (1, HCH), (1, 1))))
            done(dve.tensor_copy(hid_sq[:, :, 0:PT], free(par128[0][:, P128["b3"]:P128["b3"] + 1], (1, HCH), (0, PT))))
            for L in (0, 1):
                p = par96[L]
                done(dve.tensor_scalar(wqkv[L][:, :], p[:, P96["qkv"]:P96["qkv"] + 3 * C], p[:, P96["g1"]:P96["g1"] + 1],
                                       None, ALU.mult))
            for L in (0, 1):
                dve.wait_ge(s_wps, 3 + L)
                done(dve.tensor_tensor(brow[L][0:1, :], ps[3 + L][0:1, 0:C], rows[L][0:1, 0:C], ALU.add))
            for L in (0, 1):
                p = par96[L]
                dve.tensor_scalar(wfc1[L][:, :], p[:, P96["fc1"]:P96["fc1"] + HID], p[:, P96["g2"]:P96["g2"] + 1],
                                  None, ALU.mult)
                dve.tensor_tensor(bfc1[L][:, :], ps[L][:, 3:3 + HCH], par128[L][:, P128["bfc1"]:P128["bfc1"] + HCH], ALU.add)
                done(dve.tensor_scalar(wqkv[L][:, 0:C], wqkv[L][:, 0:C], float(HD[L]) ** -0.5, None, ALU.mult))
            for L in (0, 1):
                done(dve.tensor_copy(wfc1_high[L][:, :], wfc1[L][:, :]))
                done(dve.scalar_tensor_tensor(out=wfc1_low[L][:, :], in0=wfc1_high[L][:, :].bitcast(f32), scalar=-1.0,
                                              in1=wfc1[L][:, :], op0=ALU.mult, op1=ALU.add))
            dve.wait_ge(s_wps, 5)
            dve.tensor_tensor(wfc2[:, :, 0:C], wg3[:, :].rearrange("p (n c) -> p n c", n=HCH),
                              free(ps[2][:, 0:1], (0, HCH), (1, C)), ALU.subtract)
            dve.wait_ge(s_wps, 6)
            for L in (0, 1):
                dve.tensor_copy(bfc2[L][:, :], ps[5 + L][0:PT, 0:C])
            done(dve.tensor_copy(t_high[:, :], t_in[:, :]))
            dve.tensor_copy(tleft[:, :], tleft_in[:, :])
            done(dve.scalar_tensor_tensor(out=table[:, :], in0=t_high[:, :].bitcast(f32), scalar=tlow[:, 0:1], in1=t_in[:, :],
                                          op0=ALU.mult, op1=ALU.add))

            def stats(x, n, src, ready, ready_per):
                if not x.exists(ns):
                    return
                dve.wait_ge(ready, x.count(ready_per, ready_per))
                if x.back().exists(ns):
                    dve.wait_ge(s_xn[n], x.back().count(1, 1))
                for p in range(PAIRS):
                    ins = dve.bn_stats(bn[n][:, p, :], src[:, p, :])
                ins.then_inc(s_bn[n], 1)
                dve.wait_ge(s_bn[n], x.count(2, 1))
                dve.memset(gate[:, :], 0.0)
                for p in range(PAIRS):
                    ins = dve.bn_aggr(mv[n][:, p, :], bn[n][:, p, :])
                ins.then_inc(s_bn[n], 1)
                dve.wait_ge(s_bn[n], x.count(2, 2))
                dve.tensor_scalar(var_eps[n][:, :], free(mv[n][:, 0, 1:2], (2, PAIRS)), EPS, None, ALU.add)\
                   .then_inc(s_var[n], 1)

            def v_out(x, L, half):
                if not x.exists(ns):
                    return
                dve.wait_ge(s_v[L], x.count(2, half + 1))
                if x.back().exists(ns):
                    dve.wait_ge(s_pv[L], x.back().count(UNITS[L], UNITS[L]))
                g = ps[bank_of[("va", "vb")[half] + str(L)]][0:PT, 0:1]
                base = vM[L][:, 4 * half, 0, 0:1]
                if L == 0:
                    n = 2 * HD[0]
                    src, dst = free(g, (n, 8), (1, n)), free(base, (VW[0], 8), (1, n))
                    mask = free(vmask[:, 0:1], (0, 8), (1, n))
                else:
                    n = 2 * HD[1]
                    src = free(g, (3 * n, 8), (n, 3), (1, n))
                    dst = free(base, (3 * VW[1], 8), (VW[1] + n, 3), (1, n))
                    mask = free(vmask[:, 2 * HD[0]:2 * HD[0] + 1], (0, 8), (0, 3), (1, n))
                dve.tensor_tensor(dst, src, mask, ALU.mult).then_inc(s_vm[L], 1)

            def norm(x, n, src):
                if not x.exists(ns):
                    return
                dve.wait_ge(s_rstd[n], x.count(1, 1))
                if x.back().exists(ns):
                    dve.wait_ge(s_xt[n], x.back().count(1, 1))
                for p in range(PAIRS):
                    ins = dve.tensor_scalar(xn[n][:, p, :], src[:, p, :], mv[n][:, p, 0:1], rstd[n][:, p:p + 1],
                                            ALU.subtract, ALU.mult)
                ins.then_inc(s_xn[n], 1)

            def low_part(x, L):
                if x.exists(ns):
                    dve.wait_ge(s_xe[f"M{L}"], x.count(1, 1))
                    if x.back().exists(ns):
                        dve.wait_ge(s_f1[L], x.back().count(HCH, HCH))
                    dve.tensor_tensor(xnT_low[L][:, :], ps[bank_of[f"xtM{L}"]][0:C, 0:ST], xnT_high[L][:, :].bitcast(f32),
                                      ALU.subtract).then_inc(s_xl[L], 1)

            def variants(x, L):
                if not x.exists(ns):
                    return
                dve.wait_ge(s_ke[L], x.count(1, 1))
                if x.back().exists(ns):
                    dve.wait_ge(s_s[L], x.back().count(UNITS[L], UNITS[L]))
                for m in range(4):
                    ins = dve.tensor_scalar(kM[L][:, m, :], kT[L][:, :], kmask[:, 4 * L + m:4 * L + m + 1], None, ALU.mult)
                ins.then_inc(s_km[L], 1)

            def shift(x, L, u):
                if not x.exists(ns):
                    return
                _, _, buf = unit_place(L, u)
                if free_from := before(x, SHIFTS, unit_over(s_ex), buffer, (L, u)):
                    dve.wait_ge(*free_from)
                dve.wait_ge(s_s[L], x.count(UNITS[L], u + 1))
                s = ps[bank_of[f"sc{L}{u}"]][0:SP, 0:8 * TOK].rearrange("p (h k) -> p h k", k=TOK)
                nm = negmax[buf]
                dve.tensor_reduce(nm[:, :], s, AX.X, ALU.max, negate=True).then_inc(s_mx[L], 1)
                dve.wait_ge(s_mx[L], x.count(UNITS[L], u + 1))
                dve.tensor_tensor(shifted[buf][:, :].rearrange("p (h k) -> p h k", k=TOK), s,
                                  free(nm[:, 0:1], (1, 8), (0, TOK)), ALU.add).then_inc(s_sh[L], 1)

            def invert_den(x, L):
                if x.exists(ns):
                    dve.wait_ge(s_dt[L], x.count(1, 1))
                    if x.back().exists(ns):
                        dve.wait_ge(s_wd[L], x.back().count(1, 1))
                    g = ps[bank_of[f"dt{L}"]][0:PT, TCH:TCH + 1]
                    dve.reciprocal(rden[L][:, :, :].rearrange("p (a t) h -> p a t h", t=2),
                                   free(g, (OROWS, PAIRS), (64, 2), (1, NH[L] // 2))).then_inc(s_rd[L], 1)

            def normalise(x, L):
                if x.exists(ns):
                    dve.wait_ge(s_sp[L], x.count(1, 1))
                    if x.back().exists(ns):
                        dve.wait_ge(s_pj[L], x.back().count(1, 1))
                    dve.tensor_tensor(o_norm[L][:, :], o_raw[L][:, :], ps[bank_of[f"sp{L}"]][0:OROWS, 0:ST], ALU.mult)\
                       .then_inc(s_on[L], 1)

            def residual(x, L):
                if x.exists(ns):
                    dve.wait_ge(s_pj[L], x.count(1, 1))
                    if x.back().exists(ns):
                        dve.wait_ge(s_xb[L], x.back().count(1, 1))
                    if L == 1:
                        dve.wait_ge(s_keep, x.count(1, 1))
                    g = ps[bank_of[f"pj{L}"]][0:PT, 0:PAIRS * C].rearrange("p (n c) -> p n c", c=C)
                    dst, src = ((x_mid0, x_in), (x_mid1, x_keep))[L]
                    dve.tensor_tensor(dst[:, :, :], src[:, :, :], g, ALU.add).then_inc(s_xo[L], 1)

            def finish1(x):
                if x.exists(ns):
                    dve.wait_ge(s_f2[1], x.count(1, 1))
                    dve.wait_ge(s_xb[1], x.count(1, 1))
                    if x.back().exists(ns):
                        dve.wait_ge(s_store, x.back().count(16, 16))
                    g = ps[bank_of["f2_1"]][0:PT, 0:PAIRS * C].rearrange("p (n c) -> p n c", c=C)
                    dve.tensor_tensor(y_out[:, :, :], x_biased[1][:, :, :], g, ALU.add).then_inc(s_fin[1], 1)

            def third_stats(x):
                if not x.exists(ns):
                    return
                dve.wait_ge(s_f2[0], x.count(1, 1))
                g = ps[bank_of["f2_0"]]
                dve.tensor_copy(st3[:, :, :], free(g[0:PT, C:C + 1], (C + 2, PAIRS), (1, 2))).then_inc(s_v3, 1)
                dve.wait_ge(s_v3, x.count(4, 1))
                dve.scalar_tensor_tensor(out=var3[:, :], in0=st3[:, :, 0], scalar=-1.0, in1=st3[:, :, 0],
                                         op0=ALU.mult, op1=ALU.mult).then_inc(s_v3, 1)
                dve.wait_ge(s_v3, x.count(4, 2))
                dve.tensor_tensor(var3[:, :], var3[:, :], st3[:, :, 1], ALU.add).then_inc(s_v3, 1)
                dve.wait_ge(s_v3, x.count(4, 3))
                dve.tensor_scalar(var3[:, :], var3[:, :], 0.0, EPS, ALU.max, ALU.add).then_inc(s_v3, 1)

            def finish0(x):
                if not x.exists(ns):
                    return
                g = ps[bank_of["f2_0"]]
                dve.wait_ge(s_rstd3, x.count(1, 1))
                dve.wait_ge(s_xb[0], x.count(1, 1))
                if x.back().exists(ns):
                    dve.wait_ge(s_keep, x.back().count(1, 1))
                for p in range(PAIRS):
                    ins = dve.scalar_tensor_tensor(out=x_next[:, p, :], in0=g[0:PT, p * (C + 2):p * (C + 2) + C],
                                                   scalar=rstd3[:, p:p + 1], in1=x_biased[0][:, p, :],
                                                   op0=ALU.mult, op1=ALU.add)
                ins.then_inc(s_fin[0], 1)

            def body(i):
                s0, s1, s2, s3, s4 = Strip(i, 0), Strip(i, 1), Strip(i, 2), Strip(i, 3), Strip(i, 4)
                shift(s3, 1, 4)
                finish1(s4)
                shift(s3, 1, 5)
                variants(s1, 0)
                third_stats(s2)
                shift(s1, 0, 0)
                finish0(s2)
                stats(s2, "A1", x_next, s_fin[0], 1)
                invert_den(s3, 1)
                v_out(s1, 0, 0)
                norm(s2, "A1", x_next)
                normalise(s3, 1)
                shift(s1, 0, 1)
                residual(s3, 1)
                v_out(s1, 0, 1)
                stats(s3, "M1", x_mid1, s_xo[1], 1)
                variants(s2, 1)
                norm(s3, "M1", x_mid1)
                v_out(s2, 1, 0)
                invert_den(s1, 0)
                shift(s2, 1, 0)
                low_part(s3, 1)
                normalise(s1, 0)
                shift(s2, 1, 1)
                residual(s1, 0)
                stats(s1, "M0", x_mid0, s_xo[0], 1)
                shift(s2, 1, 2)
                norm(s1, "M0", x_mid0)
                v_out(s2, 1, 1)
                low_part(s1, 0)
                stats(s0, "A0", x_in, s_load, 16)
                shift(s2, 1, 3)
                norm(s0, "A0", x_in)

            iterate(dve, body)

        @block.gpsimd
        def _(pool):
            def inverse_root(x, n):
                if x.exists(ns):
                    pool.wait_ge(s_var[n], x.count(1, 1))
                    if x.back().exists(ns):
                        pool.wait_ge(s_xn[n], x.back().count(1, 1))
                    pool.tensor_tensor(rstd[n][:, :], var_eps[n][:, :], minus_half[:, :], ALU.pow).then_inc(s_rstd[n], 1)

            def add_bias(x, L, src):
                if x.exists(ns):
                    pool.wait_ge(s_xo[L], x.count(1, 1))
                    if x.back().exists(ns):
                        pool.wait_ge(s_fin[L], x.back().count(1, 1))
                    pool.tensor_tensor(x_biased[L][:, :, :], src[:, :, :], free(bfc2[L][:, 0:1], (0, PAIRS), (1, C)), ALU.add)\
                        .then_inc(s_xb[L], 1)

            def squares(x):
                if not x.exists(ns):
                    return
                pool.wait_ge(s_ge[0], x.count(HCH, HCH))
                if x.back().exists(ns):
                    pool.wait_ge(s_f2[0], x.back().count(1, 1))
                pool.tensor_tensor(hid_sq[:, :, :], hid[0][:, :, :], hid[0][:, :, :], ALU.mult).then_inc(s_sq, 1)
                pool.wait_ge(s_sq, x.count(3, 1))
                pool.tensor_tensor(hid_ss[:, :], hid_sq[:, 0, :], hid_sq[:, 1, :], ALU.add).then_inc(s_sq, 1)
                pool.wait_ge(s_sq, x.count(3, 2))
                pool.tensor_tensor(hid_ss[:, :], hid_ss[:, :], hid_sq[:, 2, :], ALU.add).then_inc(s_sq, 1)

            def rstd_of_third(x):
                if x.exists(ns):
                    pool.wait_ge(s_v3, x.count(4, 4))
                    if x.back().exists(ns):
                        pool.wait_ge(s_fin[0], x.back().count(1, 1))
                    pool.tensor_tensor(rstd3[:, :], var3[:, :], minus_half[:, :], ALU.pow).then_inc(s_rstd3, 1)

            def body(i):
                s0, s1, s2, s3 = Strip(i, 0), Strip(i, 1), Strip(i, 2), Strip(i, 3)
                add_bias(s2, 0, x_mid0)
                rstd_of_third(s2)
                inverse_root(s2, "A1")
                inverse_root(s3, "M1")
                add_bias(s3, 1, x_mid1)
                inverse_root(s1, "M0")
                inverse_root(s0, "A0")
                squares(s1)

            iterate(pool, body)


def _strips(x):
    x = np.roll(x, (-SHIFT, -SHIFT), axis=(1, 2))
    b = x.shape[0]
    x = x.reshape(b, 8, WS, PAIRS, 2, WS, C)
    return np.ascontiguousarray(x.transpose(1, 0, 4, 2, 5, 3, 6)).reshape(8 * b, PT, PAIRS * C)


def _image(y, b):
    y = y.reshape(8, b, 2, WS, WS, PAIRS, C).transpose(1, 0, 3, 5, 2, 4, 6).reshape(b, 8 * WS, 8 * WS, C)
    return np.ascontiguousarray(np.roll(y, (SHIFT, SHIFT), axis=(1, 2)))


def _table(t):
    c = np.stack(np.meshgrid(np.arange(WS), np.arange(WS), indexing="ij")).reshape(2, -1)
    rel = c[:, :, None] - c[:, None, :] + WS - 1
    return t[rel[0] * (2 * WS - 1) + rel[1]].transpose(0, 2, 1).reshape(TOK, -1)


def host_arrays(inp):
    a = {"x": _strips(inp["x"])}
    tab = np.concatenate([_table(inp["L0_conv_rpb_table"]), _table(inp["L1_conv_rel_bias_table"])], 1)
    a["tab"] = np.concatenate([tab, tab], 0)
    names = [dict(g1="ln1_g", b1="ln1_b", g2="ln2_g", b2="ln2_b", w1="fc1_w", c1="fc1_b", w2="fc2_w", c2="fc2_b"),
             dict(g1="norm1_w", b1="norm1_b", g2="norm2_w", b2="norm2_b", w1="mlp_w1", c1="mlp_b1", w2="mlp_w2", c2="mlp_b2")]
    for L in (0, 1):
        get = lambda n: inp[f"L{L}_conv_{names[L].get(n, n)}"]
        col = lambda v: v[:, None]
        a[f"par96_{L}"] = np.concatenate(
            [col(get("g1")), col(get("b1")), get("qkv_b").reshape(3, C).T, col(get("g2")), col(get("b2")),
             get("qkv_w"), get("w1"), get("proj_w")], 1)
        chunks = lambda v: v.reshape(HCH, 128).T
        norm3 = [chunks(get("ln3_g")), chunks(get("ln3_b"))] if L == 0 else [np.zeros((128, 2 * HCH), np.float32)]
        a[f"par128_{L}"] = np.concatenate(
            norm3 + [chunks(get("c1")), get("w2").reshape(HCH, 128, C).transpose(1, 0, 2).reshape(128, -1)], 1)
        a[f"rows{L}"] = np.concatenate([get("proj_b"), get("c2")])[None]
        w = np.zeros((OROWS, C), np.float32)
        w[0:TCH], w[64:64 + TCH] = get("proj_w")[:TCH], get("proj_w")[TCH:]
        a[f"wproj{L}"] = w
    a.update(shape_constants())
    return {n: np.ascontiguousarray(v) for n, v in a.items()}


def kernel(**inputs):
    import concourse.bacc as _bacc
    from concourse import mybir as _mybir
    from concourse.bass_utils import run_bass_kernel_spmd as _run

    arrays = host_arrays({n: np.asarray(v) for n, v in inputs.items()})
    nc = _bacc.Bacc("TRN2", target_bir_lowering=False, num_devices=1)
    d = {n: nc.dram_tensor(f"in_{n}", a.shape, _mybir.dt.from_np(a.dtype), kind="ExternalInput").ap()
         for n, a in arrays.items()}
    out = nc.dram_tensor("out_y", arrays["x"].shape, _mybir.dt.float32, kind="ExternalOutput").ap()
    swin_program(nc, d, out)
    r = _run(nc, [{f"in_{n}": a for n, a in arrays.items()}], core_ids=[0])
    return _image(np.asarray(r.results[0]["out_y"]), inputs["x"].shape[0])
```
